# Optimizing a Trainium2 kernel written in Bass

```python
import numpy as np
import jax
import jax.numpy as jnp

def _softmax(x, axis=-1):
    return jax.nn.softmax(x, axis=axis)

def _gelu(x):
    return jax.nn.gelu(x, approximate=True)

def _silu(x):
    return jax.nn.silu(x)

def _sigmoid(x):
    return jax.nn.sigmoid(x)

def _layernorm(x, axis=-1, eps=1e-05):
    m = jnp.mean(x, axis=axis, keepdims=True)
    v = jnp.var(x, axis=axis, keepdims=True)
    return (x - m) / jnp.sqrt(v + eps)

def _scatter_add(tgt, idx, src, axis=0):
    return tgt.at[idx].add(src)

def _segment_sum(src, seg, n):
    return jax.ops.segment_sum(src, seg, n)
kernel_name = 'mk_prb_d1_jaxref_r8_69503d'

def setup_inputs(seed: int=0):
    np.random.seed(seed)
    _w = jnp.asarray

    def _L0_attn_setup():
        import jax, jax.numpy as jnp
        import numpy as np
        EPS = 1e-06
        N_HEADS = 16

        def _inner(x, y):
            return -x[..., 0] * y[..., 0] + jnp.sum(x[..., 1:] * y[..., 1:], axis=-1)

        def _project(x):
            sp = jnp.clip(x[..., 1:], -8.0, 8.0)
            x0 = jnp.sqrt(1.0 + jnp.sum(sp ** 2, axis=-1, keepdims=True) + EPS)
            return jnp.concatenate([x0, sp], axis=-1)

        def _exp_map(x, v):
            vx = _inner(v, x)[..., None]
            v_tan = v + vx * x
            v_ns = jnp.maximum(_inner(v_tan, v_tan), 0.0)
            v_n = jnp.minimum(jnp.sqrt(v_ns + EPS)[..., None], 5.0)
            res = jnp.cosh(v_n) * x + jnp.sinh(v_n) * v_tan / (v_n + EPS)
            return _project(res)

        def _log_map(x, y):
            y = _project(y)
            xy = jnp.minimum(_inner(x, y)[..., None], -(1.0 + EPS))
            d = jnp.maximum(jnp.arccosh(jnp.maximum(-xy, 1.0 + EPS)), 0.001)
            direc = y + xy * x
            dn = jnp.sqrt(jnp.maximum(_inner(direc, direc), EPS))[..., None]
            return d * direc / (dn + EPS)
        key = jax.random.key(seed)
        ks = jax.random.split(key, 5)
        B, T, d = (2, 128, 128)
        x = jax.random.normal(ks[0], (B, T, d), dtype=jnp.float32)
        s = 0.02
        Wq = jax.random.normal(ks[1], (d, d), dtype=jnp.float32) * s
        Wk = jax.random.normal(ks[2], (d, d), dtype=jnp.float32) * s
        Wv = jax.random.normal(ks[3], (d, d), dtype=jnp.float32) * s
        Wo = jax.random.normal(ks[4], (d, d), dtype=jnp.float32) * s
        return {'x': x, 'Wq': Wq, 'Wk': Wk, 'Wv': Wv, 'Wo': Wo}
    _L0_attn_in = _L0_attn_setup()

    def _L0_ffn_setup():
        import jax, jax.numpy as jnp
        import numpy as np
        TOP_K = 2
        key = jax.random.key(seed)
        k0, k1, k2, k3, k4 = jax.random.split(key, 5)
        B, S, H, I, E = (4, 256, 128, 352, 8)
        s_h = 1.0 / np.sqrt(H)
        s_i = 1.0 / np.sqrt(I)
        return {'x': jax.random.normal(k0, (B, S, H), jnp.float32), 'w_router': jax.random.normal(k1, (E, H), jnp.float32) * s_h, 'w_gate': jax.random.normal(k2, (E, I, H), jnp.float32) * s_h, 'w_up': jax.random.normal(k3, (E, I, H), jnp.float32) * s_h, 'w_down': jax.random.normal(k4, (E, H, I), jnp.float32) * s_i}
    _L0_ffn_in = _L0_ffn_setup()
    _d = {'L0_attn_x': _L0_attn_in['x'], 'L0_attn_Wq': _L0_attn_in['Wq'], 'L0_attn_Wk': _L0_attn_in['Wk'], 'L0_attn_Wv': _L0_attn_in['Wv'], 'L0_attn_Wo': _L0_attn_in['Wo'], 'L0_ffn_w_router': _L0_ffn_in['w_router'], 'L0_ffn_w_gate': _L0_ffn_in['w_gate'], 'L0_ffn_w_up': _L0_ffn_in['w_up'], 'L0_ffn_w_down': _L0_ffn_in['w_down']}
    _x0 = _d['L0_attn_x']
    _d['L0_attn_x'] = jax.random.normal(jax.random.fold_in(jax.random.key(seed), 1), (4, 1024, 128), dtype=_x0.dtype)
    del _x0
    return _d

def reference(L0_attn_x, L0_attn_Wq, L0_attn_Wk, L0_attn_Wv, L0_attn_Wo, L0_ffn_w_router, L0_ffn_w_gate, L0_ffn_w_up, L0_ffn_w_down):

    def _L0_attn_ref(x, Wq, Wk, Wv, Wo):
        import jax, jax.numpy as jnp
        import numpy as np
        EPS = 1e-06
        N_HEADS = 16

        def _inner(x, y):
            return -x[..., 0] * y[..., 0] + jnp.sum(x[..., 1:] * y[..., 1:], axis=-1)

        def _project(x):
            sp = jnp.clip(x[..., 1:], -8.0, 8.0)
            x0 = jnp.sqrt(1.0 + jnp.sum(sp ** 2, axis=-1, keepdims=True) + EPS)
            return jnp.concatenate([x0, sp], axis=-1)

        def _exp_map(x, v):
            vx = _inner(v, x)[..., None]
            v_tan = v + vx * x
            v_ns = jnp.maximum(_inner(v_tan, v_tan), 0.0)
            v_n = jnp.minimum(jnp.sqrt(v_ns + EPS)[..., None], 5.0)
            res = jnp.cosh(v_n) * x + jnp.sinh(v_n) * v_tan / (v_n + EPS)
            return _project(res)

        def _log_map(x, y):
            y = _project(y)
            xy = jnp.minimum(_inner(x, y)[..., None], -(1.0 + EPS))
            d = jnp.maximum(jnp.arccosh(jnp.maximum(-xy, 1.0 + EPS)), 0.001)
            direc = y + xy * x
            dn = jnp.sqrt(jnp.maximum(_inner(direc, direc), EPS))[..., None]
            return d * direc / (dn + EPS)
        B, T, d = x.shape
        h = N_HEADS
        dh = d // h
        mu = jnp.zeros((d,), dtype=x.dtype).at[0].set(1.0)
        v = _log_map(mu, x)

        def proj_h(w):
            hh = w.reshape(B, T, h, dh)
            sp = jnp.clip(hh[..., 1:], -5.0, 5.0)
            x0 = jnp.sqrt(1.0 + jnp.sum(sp ** 2, axis=-1, keepdims=True) + EPS)
            return jnp.transpose(jnp.concatenate([x0, sp], axis=-1), (0, 2, 1, 3))
        q = proj_h(v @ Wq.T)
        k = proj_h(v @ Wk.T)
        vv = jnp.transpose((v @ Wv.T).reshape(B, T, h, dh), (0, 2, 1, 3))
        sc = (-jnp.einsum('bhqi,bhki->bhqk', q[..., :1], k[..., :1]) + jnp.einsum('bhqc,bhkc->bhqk', q[..., 1:], k[..., 1:])) / dh ** 0.5
        at = jax.nn.softmax(sc, axis=-1)
        out = jnp.einsum('bhqk,bhkc->bhqc', at, vv)
        out = jnp.transpose(out, (0, 2, 1, 3)).reshape(B, T, d)
        return _project(_exp_map(mu, out @ Wo.T))

    def _L0_ffn_ref(x, w_router, w_gate, w_up, w_down):
        import jax, jax.numpy as jnp
        import numpy as np
        TOP_K = 2
        B, S, H = x.shape
        E = w_router.shape[0]
        xf = x.reshape(-1, H)
        logits = jnp.einsum('th,eh->te', xf, w_router)
        probs = jax.nn.softmax(logits, axis=-1)
        topw, topi = jax.lax.top_k(probs, TOP_K)
        topw = topw / jnp.sum(topw, axis=-1, keepdims=True)
        onehot = (topi[..., None] == jnp.arange(E)).astype(x.dtype)
        combine = jnp.einsum('tk,tke->te', topw, onehot)
        gate = jax.nn.silu(jnp.einsum('th,eih->eti', xf, w_gate))
        up = jnp.einsum('th,eih->eti', xf, w_up)
        down = jnp.einsum('eti,ehi->eth', gate * up, w_down)
        out = jnp.einsum('eth,te->th', down, combine)
        return out.reshape(B, S, H)
    x = L0_attn_x
    xn = _layernorm(x, axis=-1)
    x = x + _L0_attn_ref(xn, L0_attn_Wq, L0_attn_Wk, L0_attn_Wv, L0_attn_Wo) + _L0_ffn_ref(xn, L0_ffn_w_router, L0_ffn_w_gate, L0_ffn_w_up, L0_ffn_w_down)
    return x

_drawn_inputs = setup_inputs


def setup_inputs(seed=0):
    import zlib

    import numpy as np

    out = dict(_drawn_inputs(seed))
    spreads = {}
    factors = {'L0_attn_Wq': 25.891, 'L0_attn_Wk': 25.079, 'L0_attn_Wv': 8.0, 'L0_attn_Wo': 8.0}
    for name, (base, spread) in spreads.items():
        noise = np.random.default_rng([zlib.crc32(name.encode()), seed]).standard_normal(out[name].shape)
        drawn = base * np.exp(spread * noise) if base else spread * noise
        out[name] = jnp.asarray(drawn.astype(out[name].dtype))
    for name, factor in factors.items():
        out[name] = (out[name] * factor).astype(out[name].dtype)
    return out
```

```python
from contextlib import ExitStack

import numpy as np

import concourse.bass as bass
from concourse import mybir

ALU = mybir.AluOpType
ACT = mybir.ActivationFunctionType
AX = mybir.AxisListType
F32 = mybir.dt.float32
BF16 = mybir.dt.bfloat16
U32 = mybir.dt.uint32
I32 = mybir.dt.int32

P = 128
B, S, D = 4, 1024, 128
JT = S // P
NT = B * JT
H, DH = 16, 8
HG = 4
NG = B * H // HG
GB = H // HG
NPART = 3
SROWS = NPART * NPART * DH
VA = DH + 1
E, I = 8, 352
ST = 256
SJ = ST // P
TOP = 2
FT = 40
IC = [(0, 128), (128, 128), (256, I - 256)]
WCOL = 2 * I + 3 * P
EPS = 1e-6
LN_EPS = 1e-5
BIG = 3.0e38
QH = 512
QKCLIP = 5.0
SHIFT = (1.0 + 2.0 * (DH - 1) * QKCLIP * QKCLIP) / (2.0 * DH ** 0.5)

NIT = NG // 2
FK = FT // NIT
STEPS = 2 * 2 * JT
GU = 3 * FK

GU_AT = {6 * k + 1 + c: 3 * k + c for k in range(FK) for c in range(3)}
_A = sorted([(6 * k, "x", k, 0) for k in range(FK)] + [(6 * k + 5, "y", k, 0) for k in range(FK)]
            + [(st, "o", n, half) for n, at in enumerate(((9, 10), (17, 19), (25, 26), (STEPS, STEPS)))
               for half, st in enumerate(at)])
A_USES = [u[1:] for u in _A]
A_AT = {st: [i for i, u in enumerate(_A) if u[0] == st] for st in {u[0] for u in _A}}


def block_program(nc, x, wqkv, wo, wr, wpack, out):
    assert FT % NIT == 0 and FT * ST >= TOP * B * S + E * (ST - 1) - ST + 1
    x_d = x.rearrange("b (p j) d -> b p j d", j=JT)
    out_d = out.rearrange("b (p j) d -> b p j d", j=JT)
    qk_d = nc.dram_tensor("qk_parts", (2, B, GB, NPART, DH * HG, S), BF16, kind="Internal").ap()
    xs_d = nc.dram_tensor("expert_in", (FT * ST, D), F32, kind="Internal").ap()
    ys_d = nc.dram_tensor("expert_out", (FT * ST, D), F32, kind="Internal").ap()
    xs_rows = xs_d.rearrange("(f p j) d -> f p j d", p=P, j=SJ)
    ys_rows = ys_d.rearrange("(f p j) d -> f p j d", p=P, j=SJ)

    with ExitStack() as ctx:
        def sb(name, shape, dt=F32):
            return ctx.enter_context(nc.sbuf_tensor(name, shape, dt))

        def sem(name):
            return ctx.enter_context(nc.semaphore(name))

        ps = ctx.enter_context(nc.psum_tensor("ps", [P, 8, 512], F32))

        x_all = sb("x_all", [P, B, JT, D])
        xn_all = sb("xn_all", [P, B, JT, D])
        v_all = sb("v_all", [P, B, JT, D])
        vaug = sb("vaug", [P, B, GB, JT, HG * VA])
        attn = sb("attn", [P, NIT, 2, JT, HG * DH])
        work = sb("work", [P, 4096])
        sq = sb("sq", [P, JT, D])
        stage = sb("stage", [P, JT, D])
        xT = sb("xT", [P, S])
        ident = sb("ident", [P, P])
        identb = sb("identb", [P, P], BF16)
        tri = sb("tri", [P, P])
        ones = sb("ones", [P, P])
        wqkv_s = sb("wqkv_s", [P, 3 * D])
        wo_s = sb("wo_s", [P, D])
        wr_s = sb("wr_s", [P, E])
        col = {n: sb("c_" + n, [P, B, JT]) for n in (
            "sum", "var", "sd", "rstd", "ss", "x0", "z", "zp", "m", "r", "a", "ln", "d", "d0", "dd", "q", "dn",
            "dne", "rec", "sc", "v0", "w1", "w2")}
        slot = [sb(f"slot{k}", [P, NT], U32) for k in range(TOP)]
        tile_expert = sb("tile_expert", [1, FT], I32)
        qst = [sb(f"qst{k}", [SROWS, HG, S], BF16) for k in range(2)]
        kst = [sb(f"kst{k}", [SROWS, HG, S], BF16) for k in range(2)]
        vst = [sb(f"vst{k}", [P, JT, HG * VA]) for k in range(2)]
        ex = sb("ex", [P, 2, HG, QH])
        orec = sb("orec", [P, 2, HG])
        w_ex = [sb(f"w_ex{k}", [P, WCOL]) for k in range(FK)]
        xs_s = [sb(f"xs_s{k}", [P, SJ, D]) for k in range(FK)]
        ys_s = [sb(f"ys_s{k}", [P, SJ, D]) for k in range(FK)]
        hT = sb("hT", [P, 3, ST])
        tiny = {n: sb("t_" + n, [P, NT]) for n in ("m1", "m2", "r1", "r2", "dm", "em", "s1")}
        iota_e = sb("iota_e", [P, E])
        iota_n = sb("iota_n", [P, B * S // ST])
        iota_t = sb("iota_t", [1, FT])
        cnt = {n: sb("n_" + n, [P, E]) for n in ("n", "tl", "ct", "off")}
        one8 = sb("one8", [P, E * NT])
        qss = sb("qss", [P, 2 * JT * GB, HG])

        qk = work[:, 0:2048].rearrange("p (j n) -> p j n", j=JT)
        rest = work[:, 2048:4096].rearrange("p (j n) -> p j n", j=JT)
        wproj = work[:, :].rearrange("p (b j d) -> p b j d", b=B, j=JT)
        parts = ex[:].rearrange("p a h q -> p (a h q)").bitcast(BF16)[:, 0:3 * 2048].rearrange(
            "p (t j n) -> p t j n", t=NPART, j=JT)
        partT = attn[:].rearrange("p a b c d -> p (a b c d)").bitcast(BF16)[:, 0:6 * S].rearrange(
            "p (n s) -> p n s", n=6)
        sqf, stf = sq[:].rearrange("p j d -> p (j d)"), stage[:].rearrange("p j d -> p (j d)")
        osb = sqf[:, 0:QH]
        th = sqf[:, QH:QH + 2 * ST].rearrange("p (a s) -> p a s", a=2)
        ga = stf[:, 0:2 * ST].rearrange("p (a s) -> p a s", a=2)
        xsT = xT[:, 0:ST]
        zeros = ex[:].rearrange("p a h q -> p (a h q)")[:, 0:1024]
        rt = {n: work[:, 256 * i:256 * (i + 1)] for i, n in enumerate(
            ("logit", "eq", "oh1", "l2", "oh2", "mask", "tot", "incl", "excl", "rk", "s1p", "s2p"))}
        te = lambda n: rt[n].rearrange("p (t e) -> p t e", e=E)
        et = lambda n: rt[n].rearrange("p (e t) -> p e t", e=E)
        cmp16 = work[:, 3072:3072 + E * iota_n.shape[1]].rearrange("p (e i) -> p e i", e=E)
        cmpt = work[0:1, 3400:3400 + FT * E].rearrange("p (f e) -> p f e", e=E)
        tef = work[0:1, 3800:3800 + FT]

        def bank(n, dt=F32):
            return ps[:, n, :] if dt == F32 else ps[:, n, :].bitcast(dt)

        two_banks = ps[:, 0:2, :].rearrange("p a b -> p (a b)")
        O_BANK, GU_BANK, MISC = 4, 5, 7

        names = """consts x_loaded w_loaded zeros_set zero_filled vaug_ones
            sum_ready xc_ready sq_ready var_ready sd_ready rstd_ready xn_ready xn_kept sp_ready sq2_ready ss_ready
            xnT_psum xnT_ready logits_psum
            chain_dve chain_act router_dve mask_ready rank_psum exp_dm slots_ready experts_ready scattered
            vbody_ready v_ready vT_psum vT_ready qkv_psum qk_evac v_evac qksq_ready qkss_ready q0_ready comp0
            p0_ready rest_ready p1_ready p2_ready partT_psum partT_ready part_stored o_zeroed
            scores_ready exp_done pv_done o_copied a_psum a_read o_rec
            gu_psum tanh_done gate_done h_ready y_gathered
            astage_ready attnT_psum attnT_ready proj_psum proj_ready wsq_ready wss_ready epi_dve epi_act
            scaled clipped fin_sq_ready fin_ss x0_ready col0_set y1_scaled y2_scaled sum1 sum2
            out_ready out_stored""".split()
        s = {n: sem(n) for n in names}
        stack_loaded = [sem(f"stack_loaded{k}") for k in range(2)]
        tile_loaded = [sem(f"tile_loaded{k}") for k in range(FK)]
        y_stored = [sem(f"y_stored{k}") for k in range(FK)]
        NSTACK = 1 + NPART + 1

        block = ctx.enter_context(nc.Block())

        @block.sync
        def _(sp):
            sp.dma_start(wr_s[:], wr).then_inc(s["w_loaded"], 16)
            sp.dma_start(x_all[:, 0], x_d[0]).then_inc(s["x_loaded"], 16)
            sp.dma_start(wqkv_s[:], wqkv).then_inc(s["w_loaded"], 16)
            sp.dma_start(wo_s[:], wo).then_inc(s["w_loaded"], 16)
            for b in range(1, B):
                sp.wait_ge(s["x_loaded"], 16 * b)
                sp.dma_start(x_all[:, b], x_d[b]).then_inc(s["x_loaded"], 16)
            sp.wait_ge(s["zeros_set"], 1)
            flat = xs_d.rearrange("(p r) d -> p (r d)", p=P)
            n = flat.shape[1] // 1024
            for i in range(n):
                sp.dma_start(flat[:, 1024 * i:1024 * (i + 1)], zeros).then_inc(s["zero_filled"], 16)

            with sp.Fori(0, B) as b:
                for n in range(2 * NPART):
                    sp.wait_ge(s["partT_ready"], b * (2 * NPART) + n + 1)
                    sp.dma_start(qk_d[n % 2, b, :, n // 2], partT[:, n, :]).then_inc(s["part_stored"], 16)

            def load_stack(g, par):
                k_rows = qk_d.rearrange("w b g t n s -> w (b g) (t n) s").rearrange("w g (tc h) s -> w g tc (h s)", h=HG)
                q_rows = qk_d.rearrange("w b g t (c h) s -> w (b g) t c (h s)", h=HG)
                sp.dma_start(kst[par][:].rearrange("r h s -> r (h s)"),
                             k_rows[1, bass.ds(g, 1)].to_broadcast((NPART, NPART * DH, HG * S))
                             ).then_inc(stack_loaded[par], 16)
                for r in range(NPART):
                    rows = slice(NPART * DH * r, NPART * DH * (r + 1))
                    sp.dma_start(qst[par][rows].rearrange("r h s -> r (h s)"),
                                 q_rows[0, g, r:r + 1].to_broadcast((NPART, DH, HG * S))
                                 ).then_inc(stack_loaded[par], 16)
                sp.dma_start(vst[par][:].rearrange("p j n -> p (j n)"),
                             vaug[:].rearrange("p b g j n -> p (b g) (j n)")[:, g, :]).then_inc(stack_loaded[par], 16)

            def load_tile(f, k):
                e = sp.value_load(tile_expert[0:1, bass.ds(f, 1)], min_val=0, max_val=E - 1)
                sp.dma_start(w_ex[k][:], wpack[e]).then_inc(tile_loaded[k], 16)
                sp.dma_start(xs_s[k][:], xs_rows[f]).then_inc(tile_loaded[k], 16)

            def store_tile(it, k):
                sp.wait_ge(s["a_read"], it * len(A_USES) + A_USES.index(("y", k, 0)) + 1)
                sp.dma_start(ys_rows[it * FK + k], ys_s[k][:]).then_inc(y_stored[k], 16)

            sp.wait_ge(s["part_stored"], 16 * 2 * NPART * B)
            sp.wait_ge(s["v_evac"], NT)
            sp.wait_ge(s["vaug_ones"], 1)
            load_stack(0, 0)
            load_stack(1, 1)
            sp.wait_ge(s["experts_ready"], 1)
            sp.wait_ge(s["scattered"], 16 * TOP * NT)
            for k in range(FK):
                load_tile(k, k)

            with sp.Fori(0, NIT - 1) as it:
                for k in range(FK):
                    store_tile(it, k)
                    load_tile(it * FK + FK + k, k)
                    if k == 2:
                        sp.wait_ge(s["pv_done"], it * 4 + 2)
                        load_stack(it * 2 + 2, 0)
                sp.wait_ge(s["pv_done"], it * 4 + 4)
                load_stack(it * 2 + 3, 1)
            for k in range(FK):
                store_tile(NIT - 1, k)

            with sp.Fori(0, B) as b:
                sp.wait_ge(s["out_ready"], b + 1)
                sp.dma_start(out_d[b], x_all[:, b]).then_inc(s["out_stored"], 16)
            sp.wait_ge(s["out_stored"], 16 * B)

        @block.gpsimd
        def _(pool):
            g = nc.gpsimd
            c = s["consts"]
            g.memset(ident[:], 0.0).then_inc(c, 1)
            g.memset(identb[:], 0.0).then_inc(c, 1)
            g.memset(tri[:], 1.0).then_inc(c, 1)
            g.memset(ones[:], 1.0).then_inc(c, 1)
            g.memset(one8[:], 1.0).then_inc(c, 1)
            pool.wait_ge(c, 5)
            eye = dict(compare_op=ALU.not_equal, fill=1.0, base=0, pattern=[[-1, P]], channel_multiplier=1)
            g.affine_select(out=ident[:], in_=ident[:], **eye).then_inc(c, 1)
            g.affine_select(out=identb[:], in_=identb[:], **eye).then_inc(c, 1)
            g.affine_select(out=tri[:], in_=tri[:], compare_op=ALU.is_gt, fill=0.0, base=0, pattern=[[1, P]],
                            channel_multiplier=-1).then_inc(c, 1)
            g.iota(iota_e[:], [[-1, E]], base=E, channel_multiplier=0,
                   allow_small_or_imprecise_dtypes=True).then_inc(c, 1)
            g.iota(iota_n[:], [[ST, iota_n.shape[1]]], base=0, channel_multiplier=0,
                   allow_small_or_imprecise_dtypes=True).then_inc(c, 1)
            g.iota(iota_t[:], [[1, FT]], base=0, channel_multiplier=0,
                   allow_small_or_imprecise_dtypes=True).then_inc(c, 1)
            g.memset(zeros, 0.0).then_inc(s["zeros_set"], 1)
            g.memset(vaug[:], 1.0).then_inc(s["vaug_ones"], 1)

            with pool.Fori(0, B) as b:
                pool.wait_ge(s["xn_ready"], b + 1)
                g.tensor_copy(xn_all[:, b], stage[:]).then_inc(s["xn_kept"], 1)

            pool.wait_ge(s["slots_ready"], TOP)
            pool.wait_ge(s["xn_kept"], B)
            pool.wait_ge(s["zero_filled"], 16 * (FT * ST * D // P // 1024))
            rows = xn_all[:].rearrange("p b j d -> p (b j) d")
            for t in range(NT):
                for k in range(TOP):
                    g.indirect_dma_start(xs_d, bass.IndirectOffsetOnAxis(ap=slot[k][:, t:t + 1], axis=0),
                                         rows[:, t, :], None).then_inc(s["scattered"], 16)

            for k in range(FK):
                pool.wait_ge(y_stored[k], 16 * NIT)
            pool.wait_ge(s["scattered"], 16 * TOP * NT)
            for t in range(NT):
                for k, dst in ((0, xn_all), (1, v_all)):
                    g.indirect_dma_start(dst[:].rearrange("p b j d -> p (b j) d")[:, t, :], None, ys_d,
                                         bass.IndirectOffsetOnAxis(ap=slot[k][:, t:t + 1], axis=0)
                                         ).then_inc(s["y_gathered"], 16)

        @block.scalar
        def _(act):
            A = nc.scalar.activation
            with act.Fori(0, B) as b:
                act.wait_ge(s["xc_ready"], b + 1)
                A(sq[:], xn_all[:, b], ACT.Square).then_inc(s["sq_ready"], 1)
                act.wait_ge(s["var_ready"], b + 1)
                A(col["sd"][:, b], col["var"][:, b], ACT.Sqrt, scale=1.0 / D, bias=LN_EPS).then_inc(s["sd_ready"], 1)
                act.wait_ge(s["sp_ready"], b + 1)
                A(sq[:, :, 1:], v_all[:, b, :, 1:], ACT.Square).then_inc(s["sq2_ready"], 1)
                act.wait_ge(s["xnT_psum"], b + 1)
                A(xT[:], two_banks, ACT.Copy).then_inc(s["xnT_ready"], 1)

            act.wait_ge(s["ss_ready"], B)
            A(col["x0"][:], col["ss"][:], ACT.Sqrt, bias=1.0 + EPS).then_inc(s["chain_act"], 1)
            act.wait_ge(s["chain_dve"], 3)
            A(col["r"][:], col["m"][:], ACT.Sqrt).then_inc(s["chain_act"], 1)
            act.wait_ge(s["chain_dve"], 7)
            A(col["dn"][:], col["q"][:], ACT.Sqrt).then_inc(s["chain_act"], 1)
            act.wait_ge(s["chain_dve"], 8)
            A(col["ln"][:], col["a"][:], ACT.Ln).then_inc(s["chain_act"], 1)
            act.wait_ge(s["mask_ready"], 2)
            A(tiny["em"][:], tiny["dm"][:], ACT.Exp).then_inc(s["exp_dm"], 1)

            act.wait_ge(s["vaug_ones"], 1)
            act.wait_ge(s["zero_filled"], 16 * (FT * ST * D // P // 1024))
            with act.Fori(0, B) as b:
                act.wait_ge(s["vT_psum"], b + 1)
                A(xT[:], two_banks, ACT.Copy).then_inc(s["vT_ready"], 1)
                for j in range(JT):
                    act.wait_ge(s["qk_evac"], b * JT + j + 1)
                    A(vaug[:, b, :, j, :].rearrange("p g (h c) -> p g h c", h=HG)[:, :, :, 0:DH],
                      bank(2 + j % 4)[:, 2 * D:3 * D].rearrange("p (g h c) -> p g h c", g=GB, h=HG),
                      ACT.Copy).then_inc(s["v_evac"], 1)
                A(work[:, 2048:4096], work[:, 0:2048], ACT.Square).then_inc(s["qksq_ready"], 1)
                act.wait_ge(s["qkss_ready"], b + 1)
                A(qss[:], qss[:], ACT.Sqrt, bias=1.0 + EPS).then_inc(s["q0_ready"], 1)
                act.wait_ge(s["comp0"], 2 * b + 2)
                A(parts[:, 0], qk, ACT.Copy).then_inc(s["p0_ready"], 1)
                act.wait_ge(s["rest_ready"], b + 1)
                A(parts[:, 1], rest, ACT.Copy).then_inc(s["p1_ready"], 1)
                act.wait_ge(s["part_stored"], b * (16 * 2 * NPART))
                for n in range(2 * NPART):
                    act.wait_ge(s["partT_psum"], b * (2 * NPART) + n + 1)
                    A(partT[:, n, :], bank(6 + n % 2, BF16), ACT.Copy).then_inc(s["partT_ready"], 1)

            with act.Fori(0, NIT) as it:
                for st in range(STEPS):
                    for hp in range(2):
                        pair = 2 * st + hp
                        act.wait_ge(s["scores_ready"], it * (2 * STEPS) + pair + 1)
                        A(ex[:, st % 2, 2 * hp:2 * hp + 2, :], ps[:, 2 * hp:2 * hp + 2, :], ACT.Exp,
                          scale=DH ** -0.5, bias=SHIFT).then_inc(s["exp_done"], 1)
                        if hp == 0 and st - 1 in GU_AT:
                            n = GU_AT[st - 1]
                            m = IC[n % 3][1]
                            act.wait_ge(s["gu_psum"], it * GU + n + 1)
                            A(th[0:m, n % 2, :], bank(GU_BANK + n % 2)[0:m, 0:ST], ACT.Tanh,
                              scale=0.5).then_inc(s["tanh_done"], 1)

            with act.Fori(0, B) as b:
                act.wait_ge(s["attnT_psum"], b + 1)
                A(xT[:], two_banks, ACT.Copy).then_inc(s["attnT_ready"], 1)
                act.wait_ge(s["proj_ready"], b + 1)
                A(sq[:, :, 1:], wproj[:, b, :, 1:], ACT.Square).then_inc(s["wsq_ready"], 1)
            act.wait_ge(s["epi_dve"], 1)
            A(col["sd"][:], col["q"][:], ACT.Sqrt).then_inc(s["epi_act"], 1)
            with act.Fori(0, B) as b:
                act.wait_ge(s["clipped"], b + 1)
                A(sq[:, :, 1:], wproj[:, b, :, 1:], ACT.Square).then_inc(s["fin_sq_ready"], 1)
                act.wait_ge(s["fin_ss"], b + 1)
                A(col["x0"][:, b], col["ss"][:, b], ACT.Sqrt, bias=1.0 + EPS).then_inc(s["x0_ready"], 1)

        @block.vector
        def _(dve):
            V = nc.vector

            def over_d(c, b):
                return c[:, b].unsqueeze(2).to_broadcast((P, JT, D))

            with dve.Fori(0, B) as b:
                dve.wait_ge(s["x_loaded"], b * 16 + 16)
                V.tensor_reduce(col["sum"][:, b], x_all[:, b], AX.X, ALU.add).then_inc(s["sum_ready"], 1)
                dve.wait_ge(s["sum_ready"], b + 1)
                V.scalar_tensor_tensor(out=xn_all[:, b], in0=over_d(col["sum"], b), scalar=-1.0 / D,
                                       in1=x_all[:, b], op0=ALU.mult, op1=ALU.add).then_inc(s["xc_ready"], 1)
                dve.wait_ge(s["sq_ready"], b + 1)
                V.tensor_reduce(col["var"][:, b], sq[:], AX.X, ALU.add).then_inc(s["var_ready"], 1)
                dve.wait_ge(s["sd_ready"], b + 1)
                V.reciprocal(col["rstd"][:, b], col["sd"][:, b]).then_inc(s["rstd_ready"], 1)
                dve.wait_ge(s["rstd_ready"], b + 1)
                dve.wait_ge(s["xn_kept"], b)
                dve.wait_ge(s["xnT_psum"], b)
                V.tensor_tensor(stage[:], xn_all[:, b], over_d(col["rstd"], b), ALU.mult).then_inc(s["xn_ready"], 1)
                dve.wait_ge(s["xn_ready"], b + 1)
                V.tensor_scalar(v_all[:, b], stage[:], 8.0, -8.0, ALU.min, ALU.max).then_inc(s["sp_ready"], 1)
                dve.wait_ge(s["sq2_ready"], b + 1)
                V.tensor_reduce(col["ss"][:, b], sq[:, :, 1:], AX.X, ALU.add).then_inc(s["ss_ready"], 1)

            done = [0]

            def link(ins):
                done[0] += 1
                ins.then_inc(s["chain_dve"], 1)
                dve.wait_ge(s["chain_dve"], done[0])

            C = {n: t[:] for n, t in col.items()}
            dve.wait_ge(s["chain_act"], 1)
            link(V.tensor_scalar(C["z"], C["x0"], 1.0 + EPS, None, ALU.max))
            link(V.tensor_scalar(C["zp"], C["z"], 1.0, None, ALU.add))
            link(V.scalar_tensor_tensor(out=C["m"], in0=C["z"], scalar=-1.0, in1=C["zp"], op0=ALU.add,
                                        op1=ALU.mult))
            link(V.tensor_tensor(C["d0"], C["x0"], C["z"], ALU.subtract))
            link(V.tensor_tensor(C["dd"], C["d0"], C["d0"], ALU.mult))
            link(V.tensor_tensor(C["dne"], C["ss"], C["dd"], ALU.subtract))
            link(V.tensor_scalar(C["q"], C["dne"], EPS, None, ALU.max))
            dve.wait_ge(s["chain_act"], 2)
            link(V.tensor_tensor(C["a"], C["z"], C["r"], ALU.add))
            dve.wait_ge(s["chain_act"], 3)
            link(V.tensor_scalar(C["dne"], C["dn"], EPS, None, ALU.add))
            link(V.reciprocal(C["rec"], C["dne"]))
            dve.wait_ge(s["chain_act"], 4)
            link(V.tensor_scalar(C["d"], C["ln"], 1e-3, None, ALU.max))
            link(V.tensor_tensor(C["sc"], C["d"], C["rec"], ALU.mult))
            link(V.tensor_tensor(C["v0"], C["sc"], C["d0"], ALU.mult))

            steps = [0]

            def R(ins):
                steps[0] += 1
                ins.then_inc(s["router_dve"], 1)
                dve.wait_ge(s["router_dve"], steps[0])

            by_e = lambda v: v.unsqueeze(2).to_broadcast((P, NT, E))
            by_t = lambda v: v.unsqueeze(2).to_broadcast((P, E, NT))
            iota_te = iota_e[:].unsqueeze(1).to_broadcast((P, NT, E))
            T = {n: t[:] for n, t in tiny.items()}
            dve.wait_ge(s["logits_psum"], B)
            dve.wait_ge(s["consts"], 11)
            R(V.tensor_copy(rt["logit"], bank(2)[:, 0:NT * E]))
            for best, oh, key, src in (("m1", "oh1", "r1", "logit"), ("m2", "oh2", "r2", "l2")):
                R(V.tensor_reduce(T[best], te(src), AX.X, ALU.max))
                R(V.tensor_tensor(te("eq"), te(src), by_e(T[best]), ALU.is_equal))
                R(V.tensor_tensor(te("eq"), te("eq"), iota_te, ALU.mult))
                R(V.tensor_reduce(T[key], te("eq"), AX.X, ALU.max))
                R(V.tensor_tensor(te(oh), iota_te, by_e(T[key]), ALU.is_equal))
                if src == "logit":
                    R(V.scalar_tensor_tensor(out=rt["l2"], in0=rt["oh1"], scalar=-BIG, in1=rt["logit"], op0=ALU.mult,
                                             op1=ALU.add))
            V.tensor_tensor(et("mask").rearrange("p e t -> p t e"), te("oh1"), te("oh2"), ALU.add
                            ).then_inc(s["mask_ready"], 1)
            V.tensor_tensor(T["dm"], T["m2"], T["m1"], ALU.subtract).then_inc(s["mask_ready"], 1)

            dve.wait_ge(s["rank_psum"], 1)
            R(V.tensor_copy(rt["tot"], bank(3)[:, 0:E * NT]))
            R(V.tensor_tensor_scan(rt["incl"], one8[:], rt["tot"], 0.0, ALU.mult, ALU.add))
            R(V.tensor_tensor(rt["excl"], rt["incl"], rt["tot"], ALU.subtract))
            N = {n: t[:] for n, t in cnt.items()}
            R(V.tensor_tensor(N["n"], et("incl")[:, :, NT - 1], et("excl")[:, :, 0], ALU.subtract))
            ni = iota_n.shape[1]
            R(V.tensor_tensor(cmp16, N["n"].unsqueeze(2).to_broadcast((P, E, ni)),
                              iota_n[:].unsqueeze(1).to_broadcast((P, E, ni)), ALU.is_gt))
            R(V.tensor_reduce(N["tl"], cmp16, AX.X, ALU.add))
            R(V.tensor_tensor_scan(N["ct"], one8[:, 0:E], N["tl"], 0.0, ALU.mult, ALU.add))
            R(V.tensor_tensor(N["off"], N["ct"], N["tl"], ALU.subtract))
            R(V.scalar_tensor_tensor(out=N["off"], in0=N["off"], scalar=float(ST), in1=et("excl")[:, :, 0],
                                     op0=ALU.mult, op1=ALU.subtract))
            R(V.tensor_tensor(et("excl"), et("excl"), by_t(N["off"]), ALU.add))
            R(V.tensor_tensor(rt["rk"], rt["excl"], bank(4)[:, 0:E * NT], ALU.add))
            rk = et("rk").rearrange("p e t -> p t e")
            for k, oh in enumerate(("oh1", "oh2")):
                R(V.tensor_tensor(te("s1p"), te(oh), rk, ALU.mult))
                R(V.tensor_reduce(T["s1"], te("s1p"), AX.X, ALU.add))
                V.tensor_copy(slot[k][:], T["s1"]).then_inc(s["slots_ready"], 1)
                dve.wait_ge(s["slots_ready"], k + 1)
            R(V.tensor_tensor(cmpt, iota_t[:].unsqueeze(2).to_broadcast((1, FT, E)),
                              N["ct"][0:1].unsqueeze(1).to_broadcast((1, FT, E)), ALU.is_ge
                              ))
            R(V.tensor_reduce(tef, cmpt, AX.X, ALU.add))
            V.tensor_scalar(tile_expert[:], tef, float(E - 1), None, ALU.min).then_inc(s["experts_ready"], 1)
            dve.wait_ge(s["exp_dm"], 1)
            W1, W2 = C["w1"].rearrange("p b j -> p (b j)"), C["w2"].rearrange("p b j -> p (b j)")
            R(V.tensor_scalar(T["s1"], T["em"], 1.0, None, ALU.add))
            R(V.reciprocal(W1, T["s1"]))
            R(V.tensor_tensor(W2, T["em"], W1, ALU.mult))
            dve.wait_ge(s["experts_ready"], 1)

            wgc = work[:, 0:2048].rearrange("p (j w g c h) -> p j w g c h", j=JT, w=2, g=GB, c=DH)
            sums = work[:, 2048:4096].rearrange("p (n c h) -> p n h c", c=DH, h=HG)[:, :, :, 1:]
            tq = qss[:].rearrange("p (j w g) h -> p j w g h", j=JT, w=2)
            dve.wait_ge(s["xn_kept"], B)
            dve.wait_ge(s["xnT_psum"], B)
            with dve.Fori(0, B) as b:
                dve.wait_ge(s["vT_psum"], b)
                V.tensor_tensor(stage[:], v_all[:, b], over_d(col["sc"], b), ALU.mult).then_inc(s["vbody_ready"], 1)
                dve.wait_ge(s["vbody_ready"], b + 1)
                V.tensor_copy(stage[:, :, 0], col["v0"][:, b]).then_inc(s["v_ready"], 1)
                for j in range(JT):
                    dve.wait_ge(s["qkv_psum"], b * JT + j + 1)
                    V.tensor_scalar(qk[:, j, :], bank(2 + j % 4)[:, 0:2 * D], QKCLIP, -QKCLIP, ALU.min, ALU.max
                                    ).then_inc(s["qk_evac"], 1)
                dve.wait_ge(s["qksq_ready"], b + 1)
                V.tensor_reduce(qss[:], sums, AX.X, ALU.add).then_inc(s["qkss_ready"], 1)
                dve.wait_ge(s["q0_ready"], b + 1)
                for j4 in range(1):
                    V.tensor_scalar(wgc[:, :, 0, :, 0, :], tq[:, :, 0], -1.0, None, ALU.mult).then_inc(s["comp0"], 1)
                    V.tensor_copy(wgc[:, :, 1, :, 0, :], tq[:, :, 1]).then_inc(s["comp0"], 1)
                dve.wait_ge(s["p0_ready"], b + 1)
                V.tensor_tensor(rest, qk, parts[:, 0], ALU.subtract).then_inc(s["rest_ready"], 1)
                dve.wait_ge(s["p1_ready"], b + 1)
                V.tensor_tensor(parts[:, 2], rest, parts[:, 1], ALU.subtract).then_inc(s["p2_ready"], 1)

            dve.wait_ge(s["v_evac"], NT)
            V.memset(bank(O_BANK), 0.0).then_inc(s["o_zeroed"], 1)

            with dve.Fori(0, NIT) as it:
                for st in range(STEPS + 1):
                    if st and st % JT == 0:
                        n = st // JT - 1
                        dve.wait_ge(s["pv_done"], it * 4 + n + 1)
                        V.tensor_copy(osb, bank(O_BANK)).then_inc(s["o_copied"], 1)
                    for use in A_AT.get(st, ()):
                        dve.wait_ge(s["a_psum"], it * len(A_USES) + use + 1)
                        kind, n, half = A_USES[use]
                        if kind == "x":
                            V.tensor_copy(xsT, bank(MISC)[:, 0:ST]).then_inc(s["a_read"], 1)
                        elif kind == "y":
                            dve.wait_ge(y_stored[n], it * 16)
                            V.tensor_copy(ys_s[n][:].rearrange("p j d -> p (j d)"), bank(MISC)[:, 0:ST]
                                          ).then_inc(s["a_read"], 1)
                        else:
                            o = bank(MISC)[:, 0:2 * P].rearrange("p (t h r) -> p t h r", t=2, h=HG)
                            V.reciprocal(orec[:], o[:, :, :, DH]).then_inc(s["o_rec"], 1)
                            dve.wait_ge(s["o_rec"], it * 8 + 2 * n + half + 1)
                            t0 = (n % 2) * 4 + half * 2
                            V.tensor_tensor(attn[:, it, n // 2, t0:t0 + 2, :].rearrange("p t (h c) -> p t h c", h=HG),
                                            o[:, :, :, 0:DH], orec[:].unsqueeze(3).to_broadcast((P, 2, HG, DH)),
                                            ALU.mult).then_inc(s["a_read"], 1)
                    if st - 1 in GU_AT:
                        n = GU_AT[st - 1]
                        m = IC[n % 3][1]
                        gu = bank(GU_BANK + n % 2)
                        dve.wait_ge(s["tanh_done"], it * GU + n + 1)
                        V.scalar_tensor_tensor(out=ga[0:m, n % 2], in0=th[0:m, n % 2], scalar=1.0, in1=gu[0:m, 0:ST],
                                               op0=ALU.add, op1=ALU.mult).then_inc(s["gate_done"], 1)
                        dve.wait_ge(s["gate_done"], it * GU + n + 1)
                        V.scalar_tensor_tensor(out=hT[0:m, n % 3], in0=ga[0:m, n % 2], scalar=0.5,
                                               in1=gu[0:m, ST:2 * ST], op0=ALU.mult, op1=ALU.mult
                                               ).then_inc(s["h_ready"], 1)

            with dve.Fori(0, B) as b:
                dve.wait_ge(s["attnT_psum"], b)
                for half in range(2):
                    V.tensor_copy(stage[:].rearrange("p j (a c d) -> p a c j d", a=2, c=2)[:, half],
                                  attn[:, b * 2 + half]).then_inc(s["astage_ready"], 1)
                dve.wait_ge(s["proj_psum"], b + 1)
                V.tensor_copy(wproj[:, b].rearrange("p j d -> p (j d)"),
                              ps[:, 2:4, :].rearrange("p a n -> p (a n)")).then_inc(s["proj_ready"], 1)
                dve.wait_ge(s["wsq_ready"], b + 1)
                V.tensor_reduce(col["ss"][:, b], sq[:, :, 1:], AX.X, ALU.add).then_inc(s["wss_ready"], 1)
            dve.wait_ge(s["wss_ready"], B)
            steps_e = [0]

            def L(ins):
                steps_e[0] += 1
                ins.then_inc(s["epi_dve"], 1)
                dve.wait_ge(s["epi_dve"], steps_e[0])

            L(V.tensor_scalar(C["q"], C["ss"], 0.0, EPS, ALU.max, ALU.add))
            dve.wait_ge(s["epi_act"], 1)
            L(V.tensor_scalar(C["z"], C["sd"], QKCLIP, None, ALU.min))
            L(V.tensor_tensor(C["m"], C["z"], C["z"], ALU.mult))
            K = 14
            L(V.tensor_scalar(C["a"], C["m"], 1.0 / ((2 * K) * (2 * K + 1)), 1.0, ALU.mult, ALU.add))
            for k in range(K - 1, 0, -1):
                L(V.tensor_tensor(C["r"], C["a"], C["m"], ALU.mult))
                L(V.tensor_scalar(C["a"], C["r"], 1.0 / ((2 * k) * (2 * k + 1)), 1.0, ALU.mult, ALU.add))
            L(V.tensor_tensor(C["d"], C["a"], C["z"], ALU.mult))
            L(V.tensor_scalar(C["dne"], C["z"], EPS, None, ALU.add))
            L(V.reciprocal(C["rec"], C["dne"]))
            L(V.tensor_tensor(C["sc"], C["d"], C["rec"], ALU.mult))

            dve.wait_ge(s["y_gathered"], 16 * TOP * NT)
            with dve.Fori(0, B) as b:
                V.tensor_tensor(wproj[:, b], wproj[:, b], over_d(col["sc"], b), ALU.mult).then_inc(s["scaled"], 1)
                dve.wait_ge(s["scaled"], b + 1)
                V.tensor_scalar(wproj[:, b], wproj[:, b], 8.0, -8.0, ALU.min, ALU.max).then_inc(s["clipped"], 1)
                V.tensor_tensor(xn_all[:, b], xn_all[:, b], over_d(col["w1"], b), ALU.mult).then_inc(s["y1_scaled"], 1)
                V.tensor_tensor(v_all[:, b], v_all[:, b], over_d(col["w2"], b), ALU.mult).then_inc(s["y2_scaled"], 1)
                dve.wait_ge(s["fin_sq_ready"], b + 1)
                V.tensor_reduce(col["ss"][:, b], sq[:, :, 1:], AX.X, ALU.add).then_inc(s["fin_ss"], 1)
                dve.wait_ge(s["y2_scaled"], b + 1)
                V.tensor_tensor(xn_all[:, b], xn_all[:, b], v_all[:, b], ALU.add).then_inc(s["sum1"], 1)
                dve.wait_ge(s["sum1"], b + 1)
                V.tensor_tensor(x_all[:, b], x_all[:, b], xn_all[:, b], ALU.add).then_inc(s["sum2"], 1)
                dve.wait_ge(s["x0_ready"], b + 1)
                V.tensor_copy(wproj[:, b, :, 0], col["x0"][:, b]).then_inc(s["col0_set"], 1)
                dve.wait_ge(s["sum2"], b + 1)
                dve.wait_ge(s["col0_set"], b + 1)
                V.tensor_tensor(x_all[:, b], x_all[:, b], wproj[:, b], ALU.add).then_inc(s["out_ready"], 1)

        @block.tensor
        def _(pe):
            M = nc.tensor.matmul

            def transposes(src):
                for j in range(JT):
                    last = nc.tensor.transpose(two_banks[:, j * P:(j + 1) * P], src[:, j, :], ident[:])
                return last

            pe.wait_ge(s["consts"], 11)
            pe.wait_ge(s["w_loaded"], 48)
            with pe.Fori(0, B) as b:
                pe.wait_ge(s["xn_ready"], b + 1)
                pe.wait_ge(s["xnT_ready"], b)
                transposes(stage).then_inc(s["xnT_psum"], 1)
                pe.wait_ge(s["xnT_ready"], b + 1)
                for j in range(JT):
                    last = M(bank(2)[:, bass.ds(b * (JT * E) + j * E, E)], xT[:, j * P:(j + 1) * P], wr_s[:],
                             start=True, stop=True)
                last.then_inc(s["logits_psum"], 1)

            pe.wait_ge(s["mask_ready"], 1)
            M(bank(3)[:, 0:E * NT], ones[:], rt["mask"], start=True, stop=True)
            M(bank(4)[:, 0:E * NT], tri[:], rt["mask"], start=True, stop=True).then_inc(s["rank_psum"], 1)

            with pe.Fori(0, B) as b:
                pe.wait_ge(s["v_ready"], b + 1)
                pe.wait_ge(s["vT_ready"], b)
                transposes(stage).then_inc(s["vT_psum"], 1)
                pe.wait_ge(s["vT_ready"], b + 1)
                for j in range(JT):
                    if j == 0 or j >= 4:
                        pe.wait_ge(s["v_evac"], b * JT + (j - 3 if j else 0))
                    M(bank(2 + j % 4)[:, 0:3 * D], xT[:, j * P:(j + 1) * P], wqkv_s[:], start=True, stop=True
                      ).then_inc(s["qkv_psum"], 1)
                for n in range(2 * NPART):
                    t, w = n // 2, n % 2
                    pe.wait_ge(s[f"p{t}_ready"], b + 1)
                    pe.wait_ge(s["partT_ready"], b * (2 * NPART) + max(n - 1, 0))
                    for j in range(JT):
                        last = nc.tensor.transpose(bank(6 + n % 2, BF16)[:, j * P:(j + 1) * P],
                                                   parts[:, t, j, w * D:(w + 1) * D], identb[:])
                    last.then_inc(s["partT_psum"], 1)

            pe.wait_ge(s["o_zeroed"], 1)
            with pe.Fori(0, NIT) as it:
                def scores(st):
                    par, qh, kb = st // (2 * JT), st // JT % 2, st % JT
                    if st % (2 * JT) == 0:
                        pe.wait_ge(stack_loaded[par], it * (16 * NSTACK) + 16 * NSTACK)
                    for hp in range(2):
                        if st:
                            pe.wait_ge(s["exp_done"], it * (2 * STEPS) + 2 * st + hp - 1)
                        for h in (2 * hp, 2 * hp + 1):
                            last = M(ps[:, h, :], kst[par][:, h, kb * P:(kb + 1) * P],
                                     qst[par][:, h, qh * QH:(qh + 1) * QH], start=True, stop=True)
                        last.then_inc(s["scores_ready"], 1)

                def weigh(st):
                    par, kb = st // (2 * JT), st % JT
                    if kb == 0:
                        pe.wait_ge(s["o_copied"], it * 4 + st // JT)
                    if st == STEPS - 1:
                        pe.wait_ge(s["exp_done"], it * (2 * STEPS) + 2 * STEPS)
                    for h in range(HG):
                        last = M(bank(O_BANK)[32 * h:32 * h + VA, :], vst[par][:, kb, h * VA:(h + 1) * VA],
                                 ex[:, st % 2, h, :], start=(kb == 0), stop=(kb == JT - 1))
                    if kb == JT - 1:
                        last.then_inc(s["pv_done"], 1)

                def last_bank(use):
                    kind, n, half = A_USES[use]
                    pe.wait_ge(s["a_read"], it * len(A_USES) + use)
                    if kind == "x":
                        pe.wait_ge(tile_loaded[n], it * 32 + 32)
                        for j in range(SJ):
                            last = nc.tensor.transpose(bank(MISC)[:, j * P:(j + 1) * P], xs_s[n][:, j, :], ident[:])
                    elif kind == "o":
                        pe.wait_ge(s["o_copied"], it * 4 + n + 1)
                        for j in range(2):
                            q0 = (2 * half + j) * P
                            last = nc.tensor.transpose(bank(MISC)[:, j * P:(j + 1) * P], osb[:, q0:q0 + P], ident[:])
                    else:
                        pe.wait_ge(s["h_ready"], it * GU + 3 * n + 3)
                        for j in range(SJ):
                            for c, (i0, m) in enumerate(IC):
                                last = M(bank(MISC)[:, j * P:(j + 1) * P], hT[0:m, c, j * P:(j + 1) * P],
                                         w_ex[n][0:m, 2 * I + c * P:2 * I + (c + 1) * P], start=(c == 0),
                                         stop=(c == 2))
                    last.then_inc(s["a_psum"], 1)

                def gate_up(n):
                    k, c = n // 3, n % 3
                    i0, m = IC[c]
                    if c == 0:
                        pe.wait_ge(s["a_read"], it * len(A_USES) + A_USES.index(("x", k, 0)) + 1)
                    if n != 1:
                        pe.wait_ge(s["h_ready"], it * GU + max(n - 1, 0))
                    for u in range(2):
                        last = M(bank(GU_BANK + n % 2)[0:m, u * ST:(u + 1) * ST],
                                 w_ex[k][:, u * I + i0:u * I + i0 + m], xsT, start=True, stop=True)
                    last.then_inc(s["gu_psum"], 1)

                for st in range(STEPS + 1):
                    if st < STEPS:
                        scores(st)
                    if st:
                        weigh(st - 1)
                    for use in A_AT.get(st, ()):
                        last_bank(use)
                    if st in GU_AT:
                        gate_up(GU_AT[st])

            pe.wait_ge(s["a_read"], NIT * len(A_USES))
            with pe.Fori(0, B) as b:
                pe.wait_ge(s["astage_ready"], b * 2 + 2)
                pe.wait_ge(s["attnT_ready"], b)
                transposes(stage).then_inc(s["attnT_psum"], 1)
                pe.wait_ge(s["attnT_ready"], b + 1)
                pe.wait_ge(s["proj_ready"], b)
                for j in range(JT):
                    last = M(ps[:, 2 + j // 4, (j % 4) * P:(j % 4 + 1) * P], xT[:, j * P:(j + 1) * P], wo_s[:],
                             start=True, stop=True)
                last.then_inc(s["proj_psum"], 1)


def kernel(L0_attn_x, L0_attn_Wq, L0_attn_Wk, L0_attn_Wv, L0_attn_Wo, L0_ffn_w_router, L0_ffn_w_gate, L0_ffn_w_up,
           L0_ffn_w_down):
    import concourse.bacc as bacc
    from concourse.bass_utils import run_bass_kernel_spmd

    a = [np.asarray(v) for v in (L0_attn_x, L0_attn_Wq, L0_attn_Wk, L0_attn_Wv, L0_attn_Wo, L0_ffn_w_router,
                                 L0_ffn_w_gate, L0_ffn_w_up, L0_ffn_w_down)]
    x, wq, wk, wv, wo, wr, wg, wu, wd = a
    gch = lambda w: w.reshape(GB, HG, DH, D).transpose(0, 2, 1, 3).reshape(D, D).T
    wqkv = np.concatenate([gch(wq), gch(wk), wv.T], axis=1)
    down = np.zeros((E, 3 * P, D), wd.dtype)
    down[:, :I] = wd.transpose(0, 2, 1)
    down = down.reshape(E, 3, P, D).transpose(0, 2, 1, 3).reshape(E, P, 3 * D)
    wpack = np.concatenate([wg.transpose(0, 2, 1), wu.transpose(0, 2, 1), down], axis=2)
    arrays = {"x": x, "wqkv": wqkv, "wo": wo.T, "wr": wr.T, "wpack": wpack}
    arrays = {k: np.ascontiguousarray(v) for k, v in arrays.items()}

    nc = bacc.Bacc("TRN2", target_bir_lowering=False, num_devices=1)
    aps = [nc.dram_tensor(k, v.shape, mybir.dt.from_np(v.dtype), kind="ExternalInput").ap() for k, v in arrays.items()]
    out = nc.dram_tensor("out", (B, S, D), F32, kind="ExternalOutput").ap()
    block_program(nc, *aps, out)
    r = run_bass_kernel_spmd(nc, [arrays], core_ids=[0])
    return r.results[0]["out"]
```

```python
from contextlib import ExitStack

import numpy as np

import concourse.bass as bass
from concourse import mybir

ALU = mybir.AluOpType
ACT = mybir.ActivationFunctionType
AX = mybir.AxisListType
F32 = mybir.dt.float32
F32R = mybir.dt.float32r
BF16 = mybir.dt.bfloat16
U32 = mybir.dt.uint32
I32 = mybir.dt.int32

P = 128
B, S, D = 4, 1024, 128
JT = S // P
HJ = JT // 2
NHB = 2 * B
NT = B * JT
H, DH = 16, 8
HG = 4
NG = B * H // HG
GB = H // HG
NPART = 3
SROWS = NPART * NPART * DH
KROWS = P
VA = DH + 1
E, I = 8, 352
ST = 256
SJ = ST // P
TOP = 2
TB = 4
YB = 2
FT = 40
IC = [(0, 128), (128, 128), (256, I - 256)]
WCOL = 2 * I + 3 * P
EPS = 1e-6
LN_EPS = 1e-5
BIG = 3.0e38
QH = 512
QKCLIP = 5.0
SHIFT = (1.0 + 2.0 * (DH - 1) * QKCLIP * QKCLIP) / (2.0 * DH ** 0.5)

NIT = NG // 2
STEPS = 2 * 2 * JT
FFN0 = 2
FK = 8
NFFN = FT // FK
GU = 3 * FK

X_AT = (0, 3, 7, 11, 15, 18, 22, 26)
Y_AT = (5, 8, 12, 16, 20, 23, 27, 31)
GU_AT = {x + 1 + c: 3 * k + c for k, x in enumerate(X_AT) for c in range(3)}


class Stage:

    def __init__(self, lo, hi, qkv=(), wo=(), logits=(), ffn=False, late=None):
        self.lo, self.hi, self.ffn, self.carry, self.last = lo, hi, ffn, lo > 0, hi == NIT
        self.qkv, self.wo, self.late, self.logits = qkv, wo, late, logits
        uses = [(8 * n + 9, "o", n) for n in range(3)]
        if self.carry:
            uses += [(1, "o", 3)]
        uses += [(st + 1, "logits", 1 + i) for i, st in enumerate(logits)]
        for i, (offset, steps, parts) in enumerate(qkv):
            uses += [(steps[0], "vT", i)] + [(st, "qkv", (i, j)) for j, st in enumerate(steps[1:])]
            uses += [(st, "part", (i, t)) for t, st in enumerate(parts)]
        for i, (offset, at, proj) in enumerate(wo):
            uses += [(at, "aT", i), (proj, "proj", i)]
        if ffn:
            uses += [(st, "x", k) for k, st in enumerate(X_AT)] + [(st, "y", k) for k, st in enumerate(Y_AT)]
        uses.sort(key=lambda u: u[0])
        self.uses = [u[1:] for u in uses]
        self.at = {st: [i for i, u in enumerate(uses) if u[0] == st] for st in range(STEPS)}
        fills = sorted([(q[1][0] - 1, "vT", i, q[0]) for i, q in enumerate(qkv)]
                       + [(w[1] - 1, "aT", i, w[0]) for i, w in enumerate(wo)])
        self.nfill = len(fills)
        self.fill = {f[0]: f[1:] for f in fills}
        self.filling = {(kind, i): n for n, (_, kind, i, _) in enumerate(fills)}

    def use(self, kind, n=0):
        return self.uses.index((kind, n))


STAGES = [
    Stage(0, 1, logits=(7, 10, 12), late=20),
    Stage(1, 2, qkv=((1, (2, 3, 4, 5, 6), (12, 14, 15)), (2, (12, 13, 14, 16, 18), (24, 26, 27))), late=28),
    Stage(2, 6, qkv=((2, (2, 4, 6, 10, 13), (19, 21, 24)),), wo=((-2, 28, 30),), ffn=True, late=26),
    Stage(6, 7, wo=((-2, 28, 30),), ffn=True, late=24),
    Stage(7, 8, wo=((-2, 2, 4), (-1, 26, 27))),
]
SPLIT_ACT = {1: "squares", 3: "roots", 5: "first", 7: "second"}
SPLIT_DVE = {2: "sums", 4: "time", 6: "rest", 8: "last"}
HEAD_USES = [("vT", 0)] + [("qkv", j) for j in range(HJ)] + [("part", t) for t in range(NPART)]
RANK_AT = 17
FIRST_TILES_AT = 22
HEAD_HB = 2
TAIL_USES = [("o", 3), ("aT", 0), ("proj", 0)]
K_SINH = 14
OUT_AT = (14, 19, 27)
EPI = ((0, 2 * JT), (2 * JT, 3 * JT), (3 * JT, 3 * JT + HJ), (3 * JT + HJ, NT))


def factorial(n):
    return 1.0 if n < 2 else n * factorial(n - 1)


def block_program(nc, x, wqkv, wo, wr, wpack, out):
    assert FT % FK == 0 and FT * ST >= TOP * B * S + E * (ST - 1) - ST + 1
    x_d = x.rearrange("b (p j) d -> b p j d", j=JT)
    out_d = out.rearrange("b (p j) d -> b p j d", j=JT)
    qk_d = nc.dram_tensor("qk_parts", (2, B, GB, NPART, DH * HG, S), BF16, kind="Internal").ap()
    v_d = nc.dram_tensor("v_aug", (B, GB, P, JT, HG * VA), F32, kind="Internal").ap()
    xs_d = nc.dram_tensor("expert_in", (FT * ST, D), F32, kind="Internal").ap()
    ys_d = nc.dram_tensor("expert_out", (FT * ST, D), F32, kind="Internal").ap()
    xs_rows = xs_d.rearrange("(f p j) d -> f p j d", p=P, j=SJ)
    ys_rows = ys_d.rearrange("(f p j) d -> f p j d", p=P, j=SJ)

    with ExitStack() as ctx:
        def sb(name, shape, dt=F32):
            return ctx.enter_context(nc.sbuf_tensor(name, shape, dt))

        def sem(name):
            return ctx.enter_context(nc.semaphore(name))

        ps = ctx.enter_context(nc.psum_tensor("ps", [P, 8, 512], F32))

        x_all = sb("x_all", [P, B, JT, D])
        xn_all = sb("xn_all", [P, B, JT, D])
        v_all = sb("v_all", [P, B, JT, D])
        attn = sb("attn", [P, NIT, 2, JT, HG * DH])
        wproj = sb("wproj", [P, NHB, HJ, D])
        osb = sb("osb", [P, QH])[:]
        th = sb("th", [P, 2, ST])[:]
        ga = sb("ga", [P, 2, ST])[:]
        rows4 = sb("rows4", [P, HJ, D])[:]
        rT = sb("rT", [P, QH])[:]
        xs_hi, xs_lo = (sb(n, [P, ST], F32R)[:] for n in ("xs_hi", "xs_lo"))
        w_hi, w_lo = (sb(n, [P, 3, 2, P], F32R)[:] for n in ("w_hi", "w_lo"))
        stats = sb("stats", [P, JT, 6])
        mv = sb("mv", [P, NT, 2])
        ident = sb("ident", [P, P])
        identb = sb("identb", [P, P], BF16)
        wqkv_s = sb("wqkv_s", [P, 3 * D])
        wo_s = sb("wo_s", [P, D])
        wr_s = sb("wr_s", [P, E])
        col = {n: sb("c_" + n, [P, B, JT]) for n in (
            "sd", "rstd", "ss", "x0", "z", "zp", "m", "r", "a", "ln", "d", "d0", "dd", "q", "dn",
            "dne", "rec", "sc", "v0", "w1", "w2")}
        slot = [sb(f"slot{k}", [P, NT], U32) for k in range(TOP)]
        tile_expert = sb("tile_expert", [1, FT], I32)
        qk = sb("qk", [P, HJ, 2 * D])
        rest = sb("rest", [P, HJ, 2 * D])
        qss = sb("qss", [P, 2 * HJ * GB, HG])
        parts = sb("parts", [P, NPART, HJ, 2 * D], BF16)
        partT = sb("partT", [P, NPART, 2, HJ * P], BF16)
        vbuf = sb("vbuf", [P, GB, HJ, HG * VA])
        qst = [sb(f"qst{k}", [KROWS, HG, S], BF16) for k in range(2)]
        kst = [sb(f"kst{k}", [KROWS, HG, S], BF16) for k in range(2)]
        vst = [sb(f"vst{k}", [P, JT, HG * VA]) for k in range(2)]
        ex = sb("ex", [P, 2, HG, QH])
        orec = sb("orec", [P, HJ, HG])
        w_ex = [sb(f"w_ex{k}", [P, WCOL]) for k in range(TB)]
        xs_s = [sb(f"xs_s{k}", [P, SJ, D]) for k in range(TB)]
        ys_s = [sb(f"ys_s{k}", [P, SJ, D]) for k in range(YB)]
        hT = sb("hT", [P, 2, 3, ST])
        tiny = {n: sb("t_" + n, [P, NT]) for n in ("m1", "m2", "r1", "r2", "dm", "em", "s1")}
        iota_e = sb("iota_e", [P, E])
        iota_n = sb("iota_n", [P, B * S // ST])
        iota_t = sb("iota_t", [1, FT])
        cnt = {n: sb("n_" + n, [P, E]) for n in ("n", "tl", "ct", "off")}
        halves = sb("halves", [P, NT - JT])
        one_eps = sb("one_eps", [P, NT - JT])
        ln_eps = sb("ln_eps", [P, NT - JT])

        vsq = w_ex[0][:, 0:S].rearrange("p (j d) -> p j d", d=D)
        xnT, zeros = w_ex[1][:, 0:S], w_ex[2][:, 0:1024]
        tri, ones, one8 = w_ex[3][:, 0:P], w_ex[3][:, P:2 * P], w_ex[3][:, 2 * P:2 * P + E * NT]
        rt = {n: wproj[:].rearrange("p a j d -> p (a j d)")[:, 256 * i:256 * (i + 1)] for i, n in enumerate(
            ("logit", "eq", "oh1", "l2", "oh2", "mask", "tot", "incl", "excl", "rk", "s1p", "cmp", "tail"))}
        te = lambda n: rt[n].rearrange("p (t e) -> p t e", e=E)
        et = lambda n: rt[n].rearrange("p (e t) -> p e t", e=E)
        ni = iota_n.shape[1]
        esq = rest[:].rearrange("p j n -> p (j n)").rearrange("p (t d) -> p t d", d=D)
        cmp16 = rt["cmp"][:, 0:E * ni].rearrange("p (e i) -> p e i", e=E)
        rest_r = wproj[:].rearrange("p a j d -> p (a j d)")[0:1, 3328:]
        cmpt = rest_r[:, 0:FT * E].rearrange("p (f e) -> p f e", e=E)
        tef = rest_r[:, FT * E:FT * E + FT]

        def bank(n, dt=F32):
            return ps[:, n, :] if dt == F32 else ps[:, n, :].bitcast(dt)

        O_BANK, GU_BANK, LENT = 4, 5, 7

        names = """consts x_loaded w_loaded zeros_set zero_filled vbuf_ones stacks_zero
            stats_ready mv_ready sd_ready rstd_ready xn_ready clipped vsq_ready ss_ready
            xnT_psum xnT_ready head_logits logits_read
            chain_dve chain_roots ln_ready plus_one router_dve mask_ready rank_psum exp_dm slots_ready experts_ready scattered
            rows_ready lent_written lent_read qksq_ready qkss_ready q0_ready comp0
            p0_ready rest_ready p1_ready p2_ready part_stored v_stored
            scores_ready exp_done pv_done o_free o_rec
            xs_hi_ready w_hi_ready w_split gu_psum tanh_done gate_done h_ready
            norm2_ready norm_ready epi_dve fss_ready x0_ready y_added out_ready out_stored""".split()
        s = {n: sem(n) for n in names}
        stack_loaded = [sem(f"stack_loaded{k}") for k in range(2)]
        tile_loaded = [sem(f"tile_loaded{k}") for k in range(TB)]
        y_stored = [sem(f"y_stored{k}") for k in range(YB)]
        y_back = [sem(f"y_back{b}") for b in range(B)]
        NSTACK = 1 + NPART + 1

        def affine(i, a, c):
            return i * a + c

        def lent_base(sg, it):
            before = HEAD_HB * len(HEAD_USES) + sum(len(t.uses) * (t.hi - t.lo) for t in STAGES if t.hi <= sg.lo)
            return lambda c: affine(it, len(sg.uses), before - sg.lo * len(sg.uses) + c)

        def rows_base(sg, it):
            before = HEAD_HB + sum(t.nfill * (t.hi - t.lo) for t in STAGES if t.hi <= sg.lo)
            return lambda c: affine(it, sg.nfill, before - sg.lo * sg.nfill + c)

        LENT_ALL = HEAD_HB * len(HEAD_USES) + sum(len(t.uses) * (t.hi - t.lo) for t in STAGES)
        ROWS_ALL = HEAD_HB + sum(t.nfill * (t.hi - t.lo) for t in STAGES)

        def run(eng, body):
            for sg in STAGES:
                if sg.hi - sg.lo == 1:
                    body(sg, sg.lo)
                else:
                    with eng.Fori(sg.lo, sg.hi) as it:
                        body(sg, it)

        block = ctx.enter_context(nc.Block())

        @block.sync
        def _(sp):
            for k in range(YB):
                sp.sem_inc(y_stored[k], 16)
            sp.dma_start(x_all[:, 0], x_d[0]).then_inc(s["x_loaded"], 16)
            sp.dma_start(wqkv_s[:], wqkv).then_inc(s["w_loaded"], 16)
            sp.dma_start(wr_s[:], wr).then_inc(s["w_loaded"], 16)
            sp.dma_start(wo_s[:], wo).then_inc(s["w_loaded"], 16)
            for b in range(1, B):
                sp.wait_ge(s["x_loaded"], 16 * b)
                sp.dma_start(x_all[:, b], x_d[b]).then_inc(s["x_loaded"], 16)

            def store_v(b, half):
                sp.dma_start(v_d.rearrange("b g p (a j) n -> b a p g (j n)", a=2)[b, half],
                             vbuf[:].rearrange("p g j n -> p g (j n)")).then_inc(s["v_stored"], 16)

            def store_part(b, half, t):
                dst = qk_d.rearrange("w b g t n (a s) -> w b t a g n s", a=2)
                for w in range(2):
                    sp.dma_start(dst[w, b, t, half], partT[:, t, w, :]).then_inc(s["part_stored"], 16)

            def load_stack(g, par):
                k_rows = qk_d.rearrange("w b g t n s -> w (b g) (t n) s").rearrange("w g (tc h) s -> w g tc (h s)", h=HG)
                q_rows = qk_d.rearrange("w b g t (c h) s -> w (b g) t c (h s)", h=HG)
                sp.dma_start(kst[par][0:SROWS].rearrange("r h s -> r (h s)"),
                             k_rows[1, bass.ds(g, 1)].to_broadcast((NPART, NPART * DH, HG * S))
                             ).then_inc(stack_loaded[par], 16)
                for r in range(NPART):
                    rows = slice(NPART * DH * r, NPART * DH * (r + 1))
                    sp.dma_start(qst[par][rows].rearrange("r h s -> r (h s)"),
                                 q_rows[0, g, r:r + 1].to_broadcast((NPART, DH, HG * S))
                                 ).then_inc(stack_loaded[par], 16)
                sp.dma_start(vst[par][:].rearrange("p j n -> p (j n)"),
                             v_d.rearrange("b g p j n -> (b g) p (j n)")[g]).then_inc(stack_loaded[par], 16)

            def load_tile(f, k):
                e = sp.value_load(tile_expert[0:1, bass.ds(f, 1)], min_val=0, max_val=E - 1)
                sp.dma_start(w_ex[k][:], wpack[e]).then_inc(tile_loaded[k], 16)
                sp.dma_start(xs_s[k][:], xs_rows[f]).then_inc(tile_loaded[k], 16)

            for hb in range(HEAD_HB):
                use = lambda kind, n: hb * len(HEAD_USES) + HEAD_USES.index((kind, n)) + 1
                sp.wait_ge(s["lent_read"], use("qkv", HJ - 1))
                store_v(hb // 2, hb % 2)
                for t in range(NPART):
                    sp.wait_ge(s["lent_read"], use("part", t))
                    store_part(hb // 2, hb % 2, t)
            sp.wait_ge(s["part_stored"], 16 * 2 * NPART * HEAD_HB)
            sp.wait_ge(s["v_stored"], 16 * HEAD_HB)
            sp.wait_ge(s["stacks_zero"], 4)
            load_stack(0, 0)
            load_stack(1, 1)
            sp.wait_ge(s["zeros_set"], 1)
            flat = xs_d.rearrange("(p r) d -> p (r d)", p=P)
            for i in range(flat.shape[1] // 1024):
                sp.dma_start(flat[:, 1024 * i:1024 * (i + 1)], zeros).then_inc(s["zero_filled"], 16)

            def iteration(sg, it):
                lent = lent_base(sg, it)
                for st in range(STEPS):
                    if st == 1 and sg.carry:
                        sp.wait_ge(s["pv_done"], it * 4)
                        load_stack(it * 2 + 1, 1)
                    if sg.ffn and st in Y_AT:
                        k = Y_AT.index(st)
                        sp.wait_ge(s["lent_read"], lent(sg.use("y", k) + 1))
                        f = affine(it, FK, k - FFN0 * FK)
                        sp.dma_start(ys_rows[f], ys_s[k % YB][:]).then_inc(y_stored[k % YB], 16)
                        if sg.hi < FFN0 + NFFN or k < FK - TB:
                            load_tile(affine(it, FK, k - FFN0 * FK + TB), k % TB)
                    if sg.hi == FFN0 and st == FIRST_TILES_AT:
                        sp.wait_ge(s["experts_ready"], 1)
                        sp.wait_ge(s["scattered"], 16 * TOP * NT)
                        for k in range(TB):
                            load_tile(k, k)
                    for i, (offset, steps, parts_at) in enumerate(sg.qkv):
                        hb = it + offset
                        if st == steps[-1]:
                            sp.wait_ge(s["lent_read"], lent(sg.use("qkv", (i, HJ - 1)) + 1))
                            store_v(hb // 2, hb % 2)
                        if st in parts_at:
                            t = parts_at.index(st)
                            sp.wait_ge(s["lent_read"], lent(sg.use("part", (i, t)) + 1))
                            store_part(hb // 2, hb % 2, t)
                    if st == sg.late:
                        sp.wait_ge(s["pv_done"], it * 4 + 2)
                        if sg.qkv:
                            sp.wait_ge(s["part_stored"], affine(it, 32 * NPART, 3 * 32 * NPART))
                            sp.wait_ge(s["v_stored"], affine(it, 16, 3 * 16))
                        load_stack(it * 2 + 2, 0)

            run(sp, iteration)
            for b in range(B):
                sp.wait_ge(s["out_ready"], b + 1)
                sp.dma_start(out_d[b], x_all[:, b]).then_inc(s["out_stored"], 16)
            sp.wait_ge(s["out_stored"], 16 * B)

        @block.gpsimd
        def _(pool):
            g = nc.gpsimd
            c = s["consts"]
            g.memset(ident[:], 0.0).then_inc(c, 1)
            g.memset(identb[:], 0.0).then_inc(c, 1)
            g.memset(tri[:], 1.0).then_inc(c, 1)
            g.memset(ones[:], 1.0).then_inc(c, 1)
            g.memset(one8[:], 1.0).then_inc(c, 1)
            g.memset(halves[:], 0.5).then_inc(c, 1)
            g.memset(one_eps[:], 1.0 + EPS).then_inc(c, 1)
            g.memset(ln_eps[:], LN_EPS).then_inc(c, 1)
            pool.wait_ge(c, 8)
            eye = dict(compare_op=ALU.not_equal, fill=1.0, base=0, pattern=[[-1, P]], channel_multiplier=1)
            g.affine_select(out=ident[:], in_=ident[:], **eye).then_inc(c, 1)
            g.affine_select(out=identb[:], in_=identb[:], **eye).then_inc(c, 1)
            g.affine_select(out=tri[:], in_=tri[:], compare_op=ALU.is_gt, fill=0.0, base=0, pattern=[[1, P]],
                            channel_multiplier=-1).then_inc(c, 1)
            g.iota(iota_e[:], [[-1, E]], base=E, channel_multiplier=0,
                   allow_small_or_imprecise_dtypes=True).then_inc(c, 1)
            g.iota(iota_n[:], [[ST, iota_n.shape[1]]], base=0, channel_multiplier=0,
                   allow_small_or_imprecise_dtypes=True).then_inc(c, 1)
            g.iota(iota_t[:], [[1, FT]], base=0, channel_multiplier=0,
                   allow_small_or_imprecise_dtypes=True).then_inc(c, 1)
            g.memset(vbuf[:], 1.0).then_inc(s["vbuf_ones"], 1)
            pool.wait_ge(s["vbuf_ones"], 1)
            for i, stack in enumerate((kst[0], qst[0], kst[1], qst[1])):
                g.memset(stack[64:KROWS], 0.0).then_inc(s["stacks_zero"], 1)
                pool.wait_ge(s["stacks_zero"], i + 1)
            g.memset(zeros, 0.0).then_inc(s["zeros_set"], 1)

            def root(out, x, done, plus=None, count=None):
                n = int(np.prod(x.shape[1:]))
                if plus is not None:
                    g.tensor_tensor(out, x, plus[:, 0:n], ALU.add).then_inc(s["plus_one"], 1)
                    pool.wait_ge(s["plus_one"], count)
                    x = out
                g.tensor_tensor(out, x, halves[:, 0:n], ALU.pow).then_inc(done, 1)

            def number(n, t0, t1):
                return col[n][:].rearrange("p b j -> p (b j)")[:, t0:t1]

            pool.wait_ge(s["mv_ready"], B)
            root(number("sd", JT, NT), mv[:, JT:NT, 1], s["sd_ready"], ln_eps, 1)
            for b in range(1, B):
                pool.wait_ge(s["clipped"], b + 1)
                pool.wait_ge(s["ss_ready"], b)
                v = v_all[:, b, :, 1:]
                g.tensor_tensor(vsq[:, :, 1:], v, v, ALU.mult).then_inc(s["vsq_ready"], 1)
            pool.wait_ge(s["ss_ready"], B)
            root(number("x0", JT, NT), number("ss", JT, NT), s["chain_roots"], one_eps, 2)
            pool.wait_ge(s["chain_dve"], 13 + 3)
            root(number("r", JT, NT), number("m", JT, NT), s["chain_roots"])
            pool.wait_ge(s["chain_dve"], 13 + 7)
            root(number("dn", JT, NT), number("q", JT, NT), s["chain_roots"])

            pool.wait_ge(s["slots_ready"], TOP)
            pool.wait_ge(s["zero_filled"], 16 * (FT * ST * D // P // 1024))
            rows = xn_all[:].rearrange("p b j d -> p (b j) d")
            for t in range(NT):
                for k in range(TOP):
                    g.indirect_dma_start(xs_d, bass.IndirectOffsetOnAxis(ap=slot[k][:, t:t + 1], axis=0),
                                         rows[:, t, :], None).then_inc(s["scattered"], 16)

            for k in range(YB):
                pool.wait_ge(y_stored[k], 16 + 16 * FT // YB)
            pool.wait_ge(s["scattered"], 16 * TOP * NT)
            for t in range(NT):
                for k, dst in ((0, xn_all), (1, v_all)):
                    g.indirect_dma_start(dst[:].rearrange("p b j d -> p (b j) d")[:, t, :], None, ys_d,
                                         bass.IndirectOffsetOnAxis(ap=slot[k][:, t:t + 1], axis=0)
                                         ).then_inc(y_back[t // JT], 16)

        @block.scalar
        def _(act):
            A = nc.scalar.activation

            def number(n, t0, t1):
                return col[n][:].rearrange("p b j -> p (b j)")[:, t0:t1]

            def deviation(t0, t1):
                act.wait_ge(s["mv_ready"], t1 // JT)
                A(number("sd", t0, t1), mv[:, t0:t1, 1], ACT.Sqrt, bias=LN_EPS).then_inc(s["sd_ready"], 1)

            def log_map(part, group, t0, t1):
                if part == "x0":
                    act.wait_ge(s["ss_ready"], t1 // JT)
                    A(number("x0", t0, t1), number("ss", t0, t1), ACT.Sqrt, bias=1.0 + EPS).then_inc(s["chain_roots"], 1)
                elif part == "roots":
                    act.wait_ge(s["chain_dve"], 13 * group + 3)
                    A(number("r", t0, t1), number("m", t0, t1), ACT.Sqrt).then_inc(s["chain_roots"], 1)
                    act.wait_ge(s["chain_dve"], 13 * group + 7)
                    A(number("dn", t0, t1), number("q", t0, t1), ACT.Sqrt).then_inc(s["chain_roots"], 1)
                else:
                    act.wait_ge(s["chain_dve"], 13 * group + 8)
                    A(number("ln", t0, t1), number("a", t0, t1), ACT.Ln).then_inc(s["ln_ready"], 1)

            deviation(0, JT)
            act.wait_ge(s["clipped"], 1)
            A(vsq[:, :, 1:], v_all[:, 0, :, 1:], ACT.Square).then_inc(s["vsq_ready"], 1)
            for part in ("x0", "roots", "log"):
                log_map(part, 0, 0, JT)

            def split(part, hb):
                if part == "squares":
                    A(rest[:], qk[:], ACT.Square).then_inc(s["qksq_ready"], 1)
                elif part == "roots":
                    act.wait_ge(s["qkss_ready"], hb + 1)
                    A(qss[:], qss[:], ACT.Sqrt, bias=1.0 + EPS).then_inc(s["q0_ready"], 1)
                elif part == "first":
                    act.wait_ge(s["comp0"], affine(hb, 2, 2))
                    A(parts[:, 0], qk[:], ACT.Copy).then_inc(s["p0_ready"], 1)
                else:
                    act.wait_ge(s["rest_ready"], hb + 1)
                    A(parts[:, 1], rest[:], ACT.Copy).then_inc(s["p1_ready"], 1)

            for hb in range(HEAD_HB):
                act.wait_ge(s["lent_read"], hb * len(HEAD_USES) + HEAD_USES.index(("qkv", HJ - 1)) + 1)
                for part in ("squares", "roots", "first", "second"):
                    split(part, hb)

            def iteration(sg, it):
                for st in range(STEPS):
                    for hp in range(2):
                        act.wait_ge(s["scores_ready"], affine(it, 2 * STEPS, 2 * st + hp + 1))
                        A(ex[:, st % 2, 2 * hp:2 * hp + 2, :], ps[:, 2 * hp:2 * hp + 2, :], ACT.Exp,
                          scale=DH ** -0.5, bias=SHIFT).then_inc(s["exp_done"], 1)
                        if hp == 0 and sg.ffn and st - 1 in GU_AT:
                            n = GU_AT[st - 1]
                            m = IC[n % 3][1]
                            act.wait_ge(s["gu_psum"], affine(it, GU, n + 1 - FFN0 * GU))
                            A(th[0:m, n % 2, :], bank(GU_BANK + n % 2)[0:m, 0:ST], ACT.Tanh,
                              scale=0.5).then_inc(s["tanh_done"], 1)
                    for i, (offset, steps, _) in enumerate(sg.qkv):
                        if st == steps[-1] + 1:
                            act.wait_ge(s["lent_read"], lent_base(sg, it)(sg.use("qkv", (i, HJ - 1)) + 1))
                        if st - steps[-1] in SPLIT_ACT:
                            split(SPLIT_ACT[st - steps[-1]], it + offset)
                    if sg.lo == 0:
                        if st == 20:
                            log_map("log", 1, JT, NT)
                        if st == 19:
                            act.wait_ge(s["mask_ready"], 2)
                            A(tiny["em"][:], tiny["dm"][:], ACT.Exp).then_inc(s["exp_dm"], 1)
                    if sg.lo == NIT - 2:
                        if st == 8:
                            norms(0)
                        if st == 19:
                            time_parts(0)
                    if sg.last:
                        if st in (6, 29):
                            norms({6: 1, 29: 2}[st])
                        if st == 12:
                            time_parts(1)

            def norms(group):
                act.wait_ge(s["norm2_ready"], group + 1)
                A(number("sd", *EPI[group]), number("q", *EPI[group]), ACT.Sqrt).then_inc(s["norm_ready"], 1)

            def time_parts(group):
                act.wait_ge(s["fss_ready"], group + 1)
                A(number("x0", *EPI[group]), number("ss", *EPI[group]), ACT.Sqrt, bias=1.0 + EPS
                  ).then_inc(s["x0_ready"], 1)

            run(act, iteration)
            time_parts(2)
            norms(3)
            time_parts(3)

        @block.vector
        def _(dve):
            V = nc.vector

            tiles = lambda v: v.rearrange("p b j d -> p (b j) d")
            number = lambda n: col[n][:].rearrange("p b j -> p (b j)")

            def token_stats(b):
                dve.wait_ge(s["x_loaded"], 16 * (b + 1))
                if b:
                    dve.wait_ge(s["mv_ready"], b)
                for j in range(JT):
                    ins = V.bn_stats(stats[:, j], x_all[:, b, j])
                ins.then_inc(s["stats_ready"], 1)
                dve.wait_ge(s["stats_ready"], b + 1)
                for j in range(JT):
                    ins = V.bn_aggr(mv[:, b * JT + j], stats[:, j])
                ins.then_inc(s["mv_ready"], 1)

            def inverse_deviation(group, t0, t1):
                dve.wait_ge(s["sd_ready"], group + 1)
                V.reciprocal(number("rstd")[:, t0:t1], number("sd")[:, t0:t1]).then_inc(s["rstd_ready"], 1)
                dve.wait_ge(s["rstd_ready"], group + 1)

            def normalise(b):
                for t in range(b * JT, (b + 1) * JT):
                    ins = V.tensor_scalar(tiles(xn_all[:])[:, t], tiles(x_all[:])[:, t], mv[:, t, 0:1],
                                          number("rstd")[:, t:t + 1], ALU.subtract, ALU.mult)
                ins.then_inc(s["xn_ready"], 1)
                dve.wait_ge(s["xn_ready"], b + 1)
                V.tensor_scalar(v_all[:, b], xn_all[:, b], 8.0, -8.0, ALU.min, ALU.max).then_inc(s["clipped"], 1)

            def turn_xn(b):
                if b:
                    dve.wait_ge(s["logits_read"], b)
                for half in range(2):
                    dve.wait_ge(s["xnT_psum"], 2 * b + half + 1)
                    V.tensor_copy(xnT[:, half * QH:(half + 1) * QH], bank(GU_BANK + half)).then_inc(s["xnT_ready"], 1)

            def keep_logits(b, src):
                return V.tensor_copy(rt["logit"][:, b * JT * E:(b + 1) * JT * E], src[:, 0:JT * E]
                                     ).then_inc(s["logits_read"], 1)

            def sum_v(b):
                dve.wait_ge(s["vsq_ready"], b + 1)
                V.tensor_reduce(col["ss"][:, b], vsq[:, :, 1:], AX.X, ALU.add).then_inc(s["ss_ready"], 1)

            done = [0]

            def link(ins):
                done[0] += 1
                ins.then_inc(s["chain_dve"], 1)
                dve.wait_ge(s["chain_dve"], done[0])

            def log_map(part, group, t0, t1):
                C = {n: number(n)[:, t0:t1] for n in col}
                if part == "first":
                    dve.wait_ge(s["chain_roots"], 3 * group + 1)
                    link(V.tensor_scalar(C["z"], C["x0"], 1.0 + EPS, None, ALU.max))
                    link(V.tensor_scalar(C["zp"], C["z"], 1.0, None, ALU.add))
                    link(V.scalar_tensor_tensor(out=C["m"], in0=C["z"], scalar=-1.0, in1=C["zp"], op0=ALU.add,
                                                op1=ALU.mult))
                    link(V.tensor_tensor(C["d0"], C["x0"], C["z"], ALU.subtract))
                    link(V.tensor_tensor(C["dd"], C["d0"], C["d0"], ALU.mult))
                    link(V.tensor_tensor(C["dne"], C["ss"], C["dd"], ALU.subtract))
                    link(V.tensor_scalar(C["q"], C["dne"], EPS, None, ALU.max))
                elif part == "second":
                    dve.wait_ge(s["chain_roots"], 3 * group + 2)
                    link(V.tensor_tensor(C["a"], C["z"], C["r"], ALU.add))
                    dve.wait_ge(s["chain_roots"], 3 * group + 3)
                    link(V.tensor_scalar(C["dne"], C["dn"], EPS, None, ALU.add))
                    link(V.reciprocal(C["rec"], C["dne"]))
                else:
                    dve.wait_ge(s["ln_ready"], group + 1)
                    link(V.tensor_scalar(C["d"], C["ln"], 1e-3, None, ALU.max))
                    link(V.tensor_tensor(C["sc"], C["d"], C["rec"], ALU.mult))
                    link(V.tensor_tensor(C["v0"], C["sc"], C["d0"], ALU.mult))

            token_stats(0)
            inverse_deviation(0, 0, JT)
            normalise(0)
            turn_xn(0)
            sum_v(0)
            for part in ("first", "second", "third"):
                log_map(part, 0, 0, JT)
            dve.wait_ge(s["head_logits"], 1)
            keep_logits(0, bank(0))

            def fill_v(hb):
                t = bass.ds(hb * HJ, HJ)
                V.tensor_tensor(rows4[:, :, 1:], tiles(v_all[:])[:, t, 1:],
                                number("sc")[:, t].unsqueeze(2).to_broadcast((P, HJ, D - 1)), ALU.mult)
                V.tensor_copy(rows4[:, :, 0], number("v0")[:, t]).then_inc(s["rows_ready"], 1)

            def read_qkv(src, j):
                V.tensor_scalar(qk[:, j, :], src[:, 0:2 * D], QKCLIP, -QKCLIP, ALU.min, ALU.max)
                V.tensor_copy(vbuf[:, :, j, :].rearrange("p g (h c) -> p g h c", h=HG)[:, :, :, 0:DH],
                              src[:, 2 * D:3 * D].rearrange("p (g h c) -> p g h c", g=GB, h=HG)
                              ).then_inc(s["lent_read"], 1)

            wgc = qk[:].rearrange("p j (w g c h) -> p j w g c h", w=2, g=GB, c=DH)
            sums = rest[:].rearrange("p j n -> p (j n)").rearrange("p (n c h) -> p n h c", c=DH, h=HG)[:, :, :, 1:]
            tq = qss[:].rearrange("p (j w g) h -> p j w g h", j=HJ, w=2)

            def split(part, hb):
                if part == "sums":
                    dve.wait_ge(s["qksq_ready"], hb + 1)
                    V.tensor_reduce(qss[:], sums, AX.X, ALU.add).then_inc(s["qkss_ready"], 1)
                elif part == "time":
                    dve.wait_ge(s["q0_ready"], hb + 1)
                    V.tensor_scalar(wgc[:, :, 0, :, 0, :], tq[:, :, 0], -1.0, None, ALU.mult).then_inc(s["comp0"], 1)
                    V.tensor_copy(wgc[:, :, 1, :, 0, :], tq[:, :, 1]).then_inc(s["comp0"], 1)
                elif part == "rest":
                    dve.wait_ge(s["p0_ready"], hb + 1)
                    V.tensor_tensor(rest[:], qk[:], parts[:, 0], ALU.subtract).then_inc(s["rest_ready"], 1)
                else:
                    dve.wait_ge(s["p1_ready"], hb + 1)
                    V.tensor_tensor(parts[:, 2], rest[:], parts[:, 1], ALU.subtract).then_inc(s["p2_ready"], 1)

            def part_copy(src, t):
                V.tensor_copy(partT[:, t].rearrange("p w s -> p (w s)"), src).then_inc(s["lent_read"], 1)

            dve.wait_ge(s["vbuf_ones"], 1)
            for hb in range(HEAD_HB):
                u0 = hb * len(HEAD_USES)
                fill_v(hb)
                for i, (kind, n) in enumerate(HEAD_USES):
                    if (kind, n) == ("part", 0):
                        for part in ("sums", "time", "rest", "last"):
                            split(part, hb)
                    dve.wait_ge(s["lent_written"], u0 + i + 1)
                    src = O_BANK + (u0 + i) % 4
                    if kind == "vT":
                        V.tensor_copy(rT, bank(src)).then_inc(s["lent_read"], 1)
                    elif kind == "qkv":
                        if n == 0 and hb:
                            dve.wait_ge(s["v_stored"], 16 * hb)
                        read_qkv(bank(src), n)
                    else:
                        if n == 0 and hb:
                            dve.wait_ge(s["part_stored"], 32 * NPART * hb)
                        part_copy(bank(src, BF16), n)

            dve.wait_ge(s["lent_read"], HEAD_HB * len(HEAD_USES))
            V.memset(bank(O_BANK), 0.0).then_inc(s["o_free"], 1)

            steps = [0]

            def R(ins):
                steps[0] += 1
                ins.then_inc(s["router_dve"], 1)
                dve.wait_ge(s["router_dve"], steps[0])

            by_e = lambda v: v.unsqueeze(2).to_broadcast((P, NT, E))
            by_t = lambda v: v.unsqueeze(2).to_broadcast((P, E, NT))
            iota_te = iota_e[:].unsqueeze(1).to_broadcast((P, NT, E))
            T = {n: t[:] for n, t in tiny.items()}
            N = {n: t[:] for n, t in cnt.items()}

            def best_expert(best, oh, key, src):
                R(V.tensor_reduce(T[best], te(src), AX.X, ALU.max))
                R(V.tensor_tensor(te("eq"), te(src), by_e(T[best]), ALU.is_equal))
                R(V.tensor_tensor(te("eq"), te("eq"), iota_te, ALU.mult))
                R(V.tensor_reduce(T[key], te("eq"), AX.X, ALU.max))
                R(V.tensor_tensor(te(oh), iota_te, by_e(T[key]), ALU.is_equal))

            def choose_first():
                dve.wait_ge(s["logits_read"], B)
                dve.wait_ge(s["consts"], 14)
                best_expert("m1", "oh1", "r1", "logit")

            def choose_second():
                R(V.scalar_tensor_tensor(out=rt["l2"], in0=rt["oh1"], scalar=-BIG, in1=rt["logit"], op0=ALU.mult,
                                         op1=ALU.add))
                best_expert("m2", "oh2", "r2", "l2")

            def choices():
                V.tensor_tensor(et("mask").rearrange("p e t -> p t e"), te("oh1"), te("oh2"), ALU.add
                                ).then_inc(s["mask_ready"], 1)
                V.tensor_tensor(T["dm"], T["m2"], T["m1"], ALU.subtract).then_inc(s["mask_ready"], 1)

            def counts():
                dve.wait_ge(s["rank_psum"], 1)
                R(V.tensor_copy(rt["tot"], bank(GU_BANK)[:, 0:E * NT]))
                R(V.tensor_tensor_scan(rt["incl"], one8[:], rt["tot"], 0.0, ALU.mult, ALU.add))
                R(V.tensor_tensor(rt["excl"], rt["incl"], rt["tot"], ALU.subtract))

            def expert_offsets():
                R(V.tensor_tensor(N["n"], et("incl")[:, :, NT - 1], et("excl")[:, :, 0], ALU.subtract))
                R(V.tensor_tensor(cmp16, N["n"].unsqueeze(2).to_broadcast((P, E, ni)),
                                  iota_n[:].unsqueeze(1).to_broadcast((P, E, ni)), ALU.is_gt))
                R(V.tensor_reduce(N["tl"], cmp16, AX.X, ALU.add))
                R(V.tensor_tensor_scan(N["ct"], one8[:, 0:E], N["tl"], 0.0, ALU.mult, ALU.add))
                R(V.tensor_tensor(N["off"], N["ct"], N["tl"], ALU.subtract))
                R(V.scalar_tensor_tensor(out=N["off"], in0=N["off"], scalar=float(ST), in1=et("excl")[:, :, 0],
                                         op0=ALU.mult, op1=ALU.subtract))

            def ranks():
                R(V.tensor_tensor(et("excl"), et("excl"), by_t(N["off"]), ALU.add))
                R(V.tensor_tensor(rt["rk"], rt["excl"], bank(GU_BANK)[:, E * NT:2 * E * NT], ALU.add))

            def slots(k, oh):
                R(V.tensor_tensor(te("s1p"), te(oh), et("rk").rearrange("p e t -> p t e"), ALU.mult))
                R(V.tensor_reduce(T["s1"], te("s1p"), AX.X, ALU.add))
                V.tensor_copy(slot[k][:], T["s1"]).then_inc(s["slots_ready"], 1)
                dve.wait_ge(s["slots_ready"], k + 1)

            def tile_experts():
                R(V.tensor_tensor(cmpt, iota_t[:].unsqueeze(2).to_broadcast((1, FT, E)),
                                  N["ct"][0:1].unsqueeze(1).to_broadcast((1, FT, E)), ALU.is_ge))
                R(V.tensor_reduce(tef, cmpt, AX.X, ALU.add))
                V.tensor_scalar(tile_expert[:], tef, float(E - 1), None, ALU.min).then_inc(s["experts_ready"], 1)

            def expert_weights():
                dve.wait_ge(s["exp_dm"], 1)
                R(V.tensor_scalar(T["s1"], T["em"], 1.0, None, ALU.add))
                R(V.reciprocal(number("w1"), T["s1"]))
                R(V.tensor_tensor(number("w2"), T["em"], number("w1"), ALU.mult))

            def first_iteration_step(st):
                if st < 3:
                    token_stats(1 + st)
                if st == 5:
                    inverse_deviation(1, JT, NT)
                if st in (5, 6, 7):
                    normalise(st - 4)
                if st in STAGES[0].logits:
                    turn_xn(1 + STAGES[0].logits.index(st))
                if st in (8, 10, 12):
                    sum_v({8: 1, 10: 2, 12: 3}[st])
                if st in (15, 19, 21):
                    log_map({15: "first", 19: "second", 21: "third"}[st], 1, JT, NT)
                if st == 13:
                    choose_first()
                if st == 14:
                    choose_second()
                if st == 15:
                    choices()
                if st == RANK_AT:
                    counts()
                if st == RANK_AT + 1:
                    expert_offsets()
                    ranks()
                if st == RANK_AT + 2:
                    slots(0, "oh1")
                if st == RANK_AT + 3:
                    slots(1, "oh2")
                if st == RANK_AT + 6:
                    tile_experts()
                    expert_weights()

            wp, xt, y1, y2 = wproj[:].rearrange("p a j d -> p (a j) d"), tiles(x_all[:]), tiles(xn_all[:]), tiles(v_all[:])
            links = [0]

            def L(ins):
                links[0] += 1
                ins.then_inc(s["epi_dve"], 1)
                dve.wait_ge(s["epi_dve"], links[0])

            def sum_squares(t0, t1):
                L(V.tensor_tensor(esq[:, 0:t1 - t0, 1:], wp[:, t0:t1, 1:], wp[:, t0:t1, 1:], ALU.mult))
                L(V.tensor_reduce(number("ss")[:, t0:t1], esq[:, 0:t1 - t0, 1:], AX.X, ALU.add))

            def norm_squares(group):
                t0, t1 = EPI[group]
                V.tensor_scalar(number("q")[:, t0:t1], number("ss")[:, t0:t1], 0.0, EPS, ALU.max, ALU.add
                                ).then_inc(s["norm2_ready"], 1)

            def sinh_factor(group):
                t0, t1 = EPI[group]
                F = {n: number(n)[:, t0:t1] for n in col}
                dve.wait_ge(s["norm_ready"], group + 1)
                L(V.tensor_scalar(F["z"], F["sd"], QKCLIP, None, ALU.min))
                L(V.tensor_tensor(F["m"], F["z"], F["z"], ALU.mult))
                L(V.tensor_scalar(F["a"], F["m"], 1.0 / factorial(2 * K_SINH + 1), None, ALU.mult))
                for k in range(K_SINH - 1, 0, -1):
                    L(V.scalar_tensor_tensor(out=F["a"], in0=F["a"], scalar=1.0 / factorial(2 * k + 1), in1=F["m"],
                                             op0=ALU.add, op1=ALU.mult))
                L(V.scalar_tensor_tensor(out=F["d"], in0=F["a"], scalar=1.0, in1=F["z"], op0=ALU.add, op1=ALU.mult))
                L(V.tensor_scalar(F["dne"], F["z"], EPS, None, ALU.add))
                L(V.reciprocal(F["rec"], F["dne"]))
                L(V.tensor_tensor(F["sc"], F["d"], F["rec"], ALU.mult))

            def scale_clip(t0, t1):
                w = wp[:, t0:t1]
                L(V.tensor_tensor(w, w, number("sc")[:, t0:t1].unsqueeze(2).to_broadcast((P, t1 - t0, D)), ALU.mult))
                L(V.tensor_scalar(w, w, 8.0, -8.0, ALU.min, ALU.max))
                sum_squares(t0, t1)

            def set_time(group):
                t0, t1 = EPI[group]
                dve.wait_ge(s["x0_ready"], group + 1)
                L(V.tensor_copy(wp[:, t0:t1, 0], number("x0")[:, t0:t1]))

            def add_attention(t0, t1):
                L(V.tensor_tensor(xt[:, t0:t1], xt[:, t0:t1], wp[:, t0:t1], ALU.add))

            def add_experts(b):
                dve.wait_ge(y_back[b], 16 * TOP * JT)
                for k, (y, w) in enumerate(((y1, "w1"), (y2, "w2"))):
                    for t in range(b * JT, (b + 1) * JT):
                        ins = V.scalar_tensor_tensor(out=xt[:, t], in0=y[:, t], scalar=number(w)[:, t:t + 1],
                                                     in1=xt[:, t], op0=ALU.mult, op1=ALU.add)
                    ins.then_inc(s["y_added"], 1)
                    dve.wait_ge(s["y_added"], b * TOP + k + 1)

            def exp_map_step(st):
                if st in (1, 2, 4, 6):
                    i = (1, 2, 4, 6).index(st)
                    sum_squares(i * HJ, (i + 1) * HJ)
                if st == 6:
                    norm_squares(0)
                if st == 9:
                    sinh_factor(0)
                if st in (10, 12, 14, 17):
                    i = (10, 12, 14, 17).index(st)
                    scale_clip(i * HJ, (i + 1) * HJ)
                if st == 18:
                    dve.sem_inc(s["fss_ready"], 1)
                if st == 20:
                    set_time(0)
                if st in (21, 22):
                    add_attention((st - 21) * JT, (st - 20) * JT)

            def last_iteration_step(st):
                t0, t1 = EPI[1]
                if st in (5, 28):
                    dve.wait_ge(s["lent_read"], lent_base(STAGES[-1], NIT - 1)(
                        sum(len(STAGES[-1].at[i]) for i in range(st))))
                if st == 5:
                    sum_squares(t0, t1)
                    norm_squares(1)
                if st == 9:
                    sinh_factor(1)
                if st in (10, 11):
                    scale_clip(t0 + (st - 10) * HJ, t0 + (st - 9) * HJ)
                if st == 11:
                    dve.sem_inc(s["fss_ready"], 1)
                if st == 13:
                    set_time(1)
                    add_attention(t0, t1)
                if st in OUT_AT:
                    add_experts(OUT_AT.index(st))
                    dve.sem_inc(s["out_ready"], 1)
                if st == 28:
                    sum_squares(*EPI[2])
                    norm_squares(2)
                if st == 30:
                    sinh_factor(2)
                if st == 31:
                    scale_clip(*EPI[2])
                    dve.sem_inc(s["fss_ready"], 1)

            def copy_sums(it, n):
                dve.wait_ge(s["pv_done"], affine(it, 4, n + 1))
                V.tensor_copy(osb, bank(O_BANK)).then_inc(s["o_free"], 1)

            def read_sums(it, n):
                o = bank(LENT).rearrange("p (t h r) -> p t h r", t=HJ, h=HG)
                V.reciprocal(orec[:], o[:, :, :, DH]).then_inc(s["o_rec"], 1)
                dve.wait_ge(s["o_rec"], affine(it, 4, n + 1))
                t0 = n % 2 * HJ
                V.tensor_tensor(attn[:, it, n // 2, t0:t0 + HJ, :].rearrange("p t (h c) -> p t h c", h=HG),
                                o[:, :, :, 0:DH], orec[:].unsqueeze(3).to_broadcast((P, HJ, HG, DH)),
                                ALU.mult).then_inc(s["lent_read"], 1)

            def fill_a(hb):
                heads = attn[:].rearrange("p (b a) c (f j) d -> p b a c f j d", a=2, f=2)
                for a in range(2):
                    ins = V.tensor_copy(rows4.rearrange("p j (a c d) -> p a c j d", a=2, c=2)[:, a],
                                        heads[:, hb // 2, a, :, hb % 2])
                ins.then_inc(s["rows_ready"], 1)

            def split_weights(it, n):
                k, (i0, m) = n // 3, IC[n % 3]
                dve.wait_ge(tile_loaded[k % TB], affine(it, 32 * FK // TB, 32 * (k // TB + 1) - FFN0 * 32 * FK // TB))
                w = w_ex[k % TB][:, 0:2 * I].rearrange("p (u i) -> p u i", u=2)[:, :, i0:i0 + m]
                V.tensor_copy(w_hi[:, n % 3, :, 0:m], w).then_inc(s["w_hi_ready"], 1)
                dve.wait_ge(s["w_hi_ready"], affine(it, GU, n + 1 - FFN0 * GU))
                V.tensor_tensor(w_lo[:, n % 3, :, 0:m], w, w_hi[:, n % 3, :, 0:m].bitcast(F32), ALU.subtract
                                ).then_inc(s["w_split"], 1)

            def iteration(sg, it):
                lent = lent_base(sg, it)
                for st in range(STEPS):
                    if st == 0 and sg.carry:
                        copy_sums(it - 1, 3)
                    if st and st % JT == 0:
                        copy_sums(it, st // JT - 1)
                    if sg.ffn and st + 1 in GU_AT:
                        split_weights(it, GU_AT[st + 1])
                    for use in sg.at[st]:
                        kind, n = sg.uses[use]
                        dve.wait_ge(s["lent_written"], lent(use + 1))
                        if kind == "x":
                            V.tensor_copy(xs_hi, bank(LENT)[:, 0:ST]).then_inc(s["xs_hi_ready"], 1)
                            dve.wait_ge(s["xs_hi_ready"], affine(it, FK, n + 1 - FFN0 * FK))
                            V.tensor_tensor(xs_lo, bank(LENT)[:, 0:ST], xs_hi.bitcast(F32), ALU.subtract
                                            ).then_inc(s["lent_read"], 1)
                        elif kind == "y":
                            dve.wait_ge(y_stored[n % YB], affine(it, 16 * FK // YB, 16 * (n // YB + 1)
                                                                 - FFN0 * 16 * FK // YB))
                            V.tensor_copy(ys_s[n % YB][:].rearrange("p j d -> p (j d)"), bank(LENT)[:, 0:ST]
                                          ).then_inc(s["lent_read"], 1)
                        elif kind == "o":
                            read_sums(it - 1 if n == 3 else it, n)
                        elif kind in ("vT", "aT"):
                            V.tensor_copy(rT, bank(LENT)).then_inc(s["lent_read"], 1)
                        elif kind == "qkv":
                            if n[1] == 0:
                                dve.wait_ge(s["v_stored"], (it + sg.qkv[n[0]][0]) * 16)
                                dve.wait_ge(s["rest_ready"], it + sg.qkv[n[0]][0])
                            read_qkv(bank(LENT), n[1])
                        elif kind == "part":
                            if n[1] == 0:
                                dve.wait_ge(s["part_stored"], (it + sg.qkv[n[0]][0]) * (32 * NPART))
                            part_copy(bank(LENT, BF16), n[1])
                        elif kind == "logits":
                            keep_logits(n, bank(LENT))
                            dve.wait_ge(s["logits_read"], n + 1)
                            dve.sem_inc(s["lent_read"], 1)
                        else:
                            V.tensor_copy(wproj[:, it + sg.wo[n][0]].rearrange("p j d -> p (j d)"), bank(LENT)
                                          ).then_inc(s["lent_read"], 1)
                    if st in sg.fill:
                        kind, n, offset = sg.fill[st]
                        if kind == "vT":
                            fill_v(it + offset)
                        else:
                            dve.wait_ge(s["lent_read"], lent(sum(len(sg.at[i]) for i in range(st + 1))))
                            fill_a(it + offset)
                    if sg.ffn and st - 1 in GU_AT:
                        n = GU_AT[st - 1]
                        m = IC[n % 3][1]
                        gu = bank(GU_BANK + n % 2)
                        dve.wait_ge(s["tanh_done"], affine(it, GU, n + 1 - FFN0 * GU))
                        V.scalar_tensor_tensor(out=ga[0:m, n % 2], in0=th[0:m, n % 2], scalar=1.0, in1=gu[0:m, 0:ST],
                                               op0=ALU.add, op1=ALU.mult).then_inc(s["gate_done"], 1)
                        dve.wait_ge(s["gate_done"], affine(it, GU, n + 1 - FFN0 * GU))
                        V.scalar_tensor_tensor(out=hT[0:m, n // 3 % 2, n % 3], in0=ga[0:m, n % 2], scalar=0.5,
                                               in1=gu[0:m, ST:2 * ST], op0=ALU.mult, op1=ALU.mult
                                               ).then_inc(s["h_ready"], 1)
                    for offset, steps_at, _ in sg.qkv:
                        if st - steps_at[-1] in SPLIT_DVE:
                            split(SPLIT_DVE[st - steps_at[-1]], it + offset)
                    if sg.lo == 0:
                        first_iteration_step(st)
                    if sg.lo == NIT - 2:
                        exp_map_step(st)
                    if sg.last:
                        last_iteration_step(st)

            run(dve, iteration)
            copy_sums(NIT - 1, 3)
            dve.wait_ge(s["lent_written"], LENT_ALL + 1)
            read_sums(NIT - 1, 3)
            dve.wait_ge(s["lent_read"], LENT_ALL + 1)
            fill_a(NHB - 1)
            dve.wait_ge(s["lent_written"], LENT_ALL + 2)
            V.tensor_copy(rT, bank(LENT)).then_inc(s["lent_read"], 1)
            dve.wait_ge(s["lent_written"], LENT_ALL + 3)
            V.tensor_copy(wproj[:, NHB - 1].rearrange("p j d -> p (j d)"), bank(LENT)).then_inc(s["lent_read"], 1)
            dve.wait_ge(s["lent_read"], LENT_ALL + 3)
            sum_squares(*EPI[3])
            norm_squares(3)
            set_time(2)
            add_attention(*EPI[2])
            add_experts(B - 1)
            sinh_factor(3)
            scale_clip(*EPI[3])
            dve.sem_inc(s["fss_ready"], 1)
            set_time(3)
            add_attention(*EPI[3])
            dve.sem_inc(s["out_ready"], 1)

        @block.tensor
        def _(pe):
            M = nc.tensor.matmul

            def transposes(dst, src, n):
                for j in range(n):
                    last = nc.tensor.transpose(dst[:, j * P:(j + 1) * P], src[:, j, :], ident[:])
                return last

            pe.wait_ge(s["consts"], 14)
            pe.wait_ge(s["w_loaded"], 48)

            def turn_xn(b):
                pe.wait_ge(s["xn_ready"], b + 1)
                if b:
                    pe.wait_ge(s["xnT_ready"], 2 * b)
                for half in range(2):
                    transposes(bank(GU_BANK + half), xn_all[:, b, half * HJ:], HJ).then_inc(s["xnT_psum"], 1)

            def logits(b, dst):
                pe.wait_ge(s["xnT_ready"], 2 * b + 2)
                for j in range(JT):
                    last = M(dst[:, j * E:(j + 1) * E], xnT[:, j * P:(j + 1) * P], wr_s[:], start=True, stop=True)
                return last

            turn_xn(0)
            logits(0, bank(0)).then_inc(s["head_logits"], 1)

            def qkv(dst, j):
                return M(dst[:, 0:3 * D], rT[:, j * P:(j + 1) * P], wqkv_s[:], start=True, stop=True)

            def part_transposes(dst, t, hb):
                pe.wait_ge(s[f"p{t}_ready"], hb + 1)
                for w in range(2):
                    for j in range(HJ):
                        last = nc.tensor.transpose(dst[:, (w * HJ + j) * P:(w * HJ + j + 1) * P],
                                                   parts[:, t, j, w * D:(w + 1) * D], identb[:])
                return last

            for hb in range(HEAD_HB):
                for i, (kind, n) in enumerate(HEAD_USES):
                    u = hb * len(HEAD_USES) + i
                    free, rows_turned = u - 3, u - i + 1
                    need = free if kind == "vT" else max(free, rows_turned)
                    if need > 0:
                        pe.wait_ge(s["lent_read"], need)
                    dst = O_BANK + u % 4
                    if kind == "vT":
                        pe.wait_ge(s["rows_ready"], hb + 1)
                        last = transposes(bank(dst), rows4, HJ)
                    elif kind == "qkv":
                        last = qkv(bank(dst), n)
                    else:
                        last = part_transposes(bank(dst, BF16), n, hb)
                    last.then_inc(s["lent_written"], 1)

            def rank():
                pe.wait_ge(s["mask_ready"], 1)
                M(bank(GU_BANK)[:, 0:E * NT], ones[:], rt["mask"], start=True, stop=True)
                M(bank(GU_BANK)[:, E * NT:2 * E * NT], tri[:], rt["mask"], start=True, stop=True
                  ).then_inc(s["rank_psum"], 1)

            def weigh(it, st):
                par, kb = st // (2 * JT), st % JT
                if kb == 0:
                    pe.wait_ge(s["o_free"], affine(it, 4, st // JT + 1))
                for h in range(HG):
                    last = M(bank(O_BANK)[32 * h:32 * h + VA, :], vst[par][:, kb, h * VA:(h + 1) * VA],
                             ex[:, st % 2, h, :], start=(kb == 0), stop=(kb == JT - 1))
                if kb == JT - 1:
                    last.then_inc(s["pv_done"], 1)

            def iteration(sg, it):
                lent, rows = lent_base(sg, it), rows_base(sg, it)

                def scores(st):
                    par, qh, kb = st // (2 * JT), st // JT % 2, st % JT
                    if st % (2 * JT) == 0:
                        pe.wait_ge(stack_loaded[par], affine(it, 16 * NSTACK, 16 * NSTACK))
                    for hp in range(2):
                        if st or sg.carry:
                            pe.wait_ge(s["exp_done"], affine(it, 2 * STEPS, 2 * st + hp - 1))
                        for h in (2 * hp, 2 * hp + 1):
                            last = M(ps[:, h, :], kst[par][:, h, kb * P:(kb + 1) * P],
                                     qst[par][:, h, qh * QH:(qh + 1) * QH], start=True, stop=True)
                        last.then_inc(s["scores_ready"], 1)

                def lent_bank(use):
                    kind, n = sg.uses[use]
                    pe.wait_ge(s["lent_read"], lent(use))
                    if kind == "x":
                        pe.wait_ge(tile_loaded[n % TB], affine(it, 32 * FK // TB, 32 * (n // TB + 1)
                                                               - FFN0 * 32 * FK // TB))
                        last = transposes(bank(LENT), xs_s[n % TB], SJ)
                    elif kind == "y":
                        pe.wait_ge(s["h_ready"], affine(it, GU, 3 * n + 3 - FFN0 * GU))
                        for j in range(SJ):
                            for c, (i0, m) in enumerate(IC):
                                last = M(bank(LENT)[:, j * P:(j + 1) * P], hT[0:m, n % 2, c, j * P:(j + 1) * P],
                                         w_ex[n % TB][0:m, 2 * I + c * P:2 * I + (c + 1) * P], start=(c == 0),
                                         stop=(c == 2))
                    elif kind == "o":
                        pe.wait_ge(s["o_free"], affine(it, 4, 1 if n == 3 else n + 2))
                        last = transposes(bank(LENT), osb.rearrange("p (j d) -> p j d", d=P), HJ)
                    elif kind in ("vT", "aT"):
                        pe.wait_ge(s["rows_ready"], rows(sg.filling[kind, n] + 1))
                        last = transposes(bank(LENT), rows4, HJ)
                    elif kind == "qkv":
                        last = qkv(bank(LENT), n[1])
                    elif kind == "part":
                        last = part_transposes(bank(LENT, BF16), n[1], it + sg.qkv[n[0]][0])
                    elif kind == "logits":
                        last = logits(n, bank(LENT))
                    else:
                        last = project()
                    last.then_inc(s["lent_written"], 1)

                def gate_up(n):
                    k, c = n // 3, n % 3
                    m = IC[c][1]
                    if c == 0:
                        pe.wait_ge(s["lent_read"], lent(sg.use("x", k) + 1))
                    if n > 1:
                        pe.wait_ge(s["h_ready"], affine(it, GU, n - 1 - FFN0 * GU))
                    pe.wait_ge(s["w_split"], affine(it, GU, n + 1 - FFN0 * GU))
                    for u in range(2):
                        hi, lo = (w[:, n % 3, u, 0:m] for w in (w_hi, w_lo))
                        for i, (w, rows) in enumerate(((hi, xs_hi), (hi, xs_lo), (lo, xs_hi))):
                            last = M(bank(GU_BANK + n % 2)[0:m, u * ST:(u + 1) * ST], w, rows,
                                     start=(i == 0), stop=(i == 2))
                    last.then_inc(s["gu_psum"], 1)

                for st in range(STEPS):
                    scores(st)
                    if st:
                        weigh(it, st - 1)
                    elif sg.carry:
                        weigh(it - 1, STEPS - 1)
                    if sg.ffn and st in GU_AT:
                        gate_up(GU_AT[st])
                    for use in sg.at[st]:
                        lent_bank(use)
                    if st in sg.logits:
                        turn_xn(1 + sg.logits.index(st))
                    if sg.lo == 0 and st == RANK_AT:
                        rank()

            def project():
                for j in range(HJ):
                    last = M(bank(LENT)[:, j * P:(j + 1) * P], rT[:, j * P:(j + 1) * P], wo_s[:], start=True, stop=True)
                return last

            run(pe, iteration)
            pe.wait_ge(s["exp_done"], NIT * 2 * STEPS)
            weigh(NIT - 1, STEPS - 1)
            pe.wait_ge(s["lent_read"], LENT_ALL)
            pe.wait_ge(s["o_free"], NIT * 4 + 1)
            transposes(bank(LENT), osb.rearrange("p (j d) -> p j d", d=P), HJ).then_inc(s["lent_written"], 1)
            pe.wait_ge(s["lent_read"], LENT_ALL + 1)
            pe.wait_ge(s["rows_ready"], ROWS_ALL + 1)
            transposes(bank(LENT), rows4, HJ).then_inc(s["lent_written"], 1)
            pe.wait_ge(s["lent_read"], LENT_ALL + 2)
            project().then_inc(s["lent_written"], 1)


def kernel(L0_attn_x, L0_attn_Wq, L0_attn_Wk, L0_attn_Wv, L0_attn_Wo, L0_ffn_w_router, L0_ffn_w_gate, L0_ffn_w_up,
           L0_ffn_w_down):
    import concourse.bacc as bacc
    from concourse.bass_utils import run_bass_kernel_spmd

    a = [np.asarray(v) for v in (L0_attn_x, L0_attn_Wq, L0_attn_Wk, L0_attn_Wv, L0_attn_Wo, L0_ffn_w_router,
                                 L0_ffn_w_gate, L0_ffn_w_up, L0_ffn_w_down)]
    x, wq, wk, wv, wo, wr, wg, wu, wd = a
    gch = lambda w: w.reshape(GB, HG, DH, D).transpose(0, 2, 1, 3).reshape(D, D).T
    wqkv = np.concatenate([gch(wq), gch(wk), wv.T], axis=1)
    down = np.zeros((E, 3 * P, D), wd.dtype)
    down[:, :I] = wd.transpose(0, 2, 1)
    down = down.reshape(E, 3, P, D).transpose(0, 2, 1, 3).reshape(E, P, 3 * D)
    wpack = np.concatenate([wg.transpose(0, 2, 1), wu.transpose(0, 2, 1), down], axis=2)
    arrays = {"x": x, "wqkv": wqkv, "wo": wo.T, "wr": wr.T, "wpack": wpack}
    arrays = {k: np.ascontiguousarray(v) for k, v in arrays.items()}

    nc = bacc.Bacc("TRN2", target_bir_lowering=False, num_devices=1)
    aps = [nc.dram_tensor(k, v.shape, mybir.dt.from_np(v.dtype), kind="ExternalInput").ap() for k, v in arrays.items()]
    out = nc.dram_tensor("out", (B, S, D), F32, kind="ExternalOutput").ap()
    block_program(nc, *aps, out)
    r = run_bass_kernel_spmd(nc, [arrays], core_ids=[0])
    return r.results[0]["out"]
```

```python
from contextlib import ExitStack

import numpy as np

import concourse.bass as bass
from concourse import mybir

ALU = mybir.AluOpType
ACT = mybir.ActivationFunctionType
AX = mybir.AxisListType
F32 = mybir.dt.float32
F32R = mybir.dt.float32r
BF16 = mybir.dt.bfloat16
U32 = mybir.dt.uint32
I32 = mybir.dt.int32

P = 128
B, S, D = 4, 1024, 128
JT = S // P
HJ = JT // 2
NHB = 2 * B
NT = B * JT
H, DH = 16, 8
HG = 4
NG = B * H // HG
GB = H // HG
NPART = 3
SROWS = NPART * NPART * DH
KROWS = P
VA = DH + 1
E, I = 8, 352
ST = 256
SJ = ST // P
TOP = 2
TB = 4
YB = 2
FT = (TOP * B * S + E * (ST - 1)) // ST
IC = [(0, 128), (128, 128), (256, I - 256)]
WCOL = 2 * I + 3 * P
EPS = 1e-6
LN_EPS = 1e-5
BIG = 3.0e38
QH = 512
QKCLIP = 5.0
SHIFT = (1.0 + 2.0 * (DH - 1) * QKCLIP * QKCLIP) / (2.0 * DH ** 0.5)

NIT = NG // 2
STEPS = 2 * 2 * JT
FFN0 = 2
FK = 8
NFFN = -(-FT // FK)
FK_LAST = FT - (NFFN - 1) * FK
GU = 3 * FK

X_AT = (0, 3, 7, 11, 14, 18, 22, 26)
Y_AT = (5, 8, 12, 16, 20, 23, 27, 31)
GU_AT = {x + 1 + c: 3 * k + c for k, x in enumerate(X_AT) for c in range(3)}


class Stage:

    def __init__(self, lo, hi, qkv=(), wo=(), logits=(), ffn=0, late=None):
        self.lo, self.hi, self.ffn, self.carry, self.last = lo, hi, ffn, lo > 0, hi == NIT
        self.qkv, self.wo, self.late, self.logits = qkv, wo, late, logits
        self.y_at, self.gu = Y_AT[:ffn], {st: n for st, n in GU_AT.items() if n < 3 * ffn}
        uses = [(8 * n + 9, "o", n) for n in range(3)]
        if self.carry:
            uses += [(1, "o", 3)]
        uses += [(st + 1, "logits", 1 + i) for i, st in enumerate(logits)]
        for i, (offset, steps, parts) in enumerate(qkv):
            uses += [(steps[0], "vT", i)] + [(st, "qkv", (i, j)) for j, st in enumerate(steps[1:])]
            uses += [(st, "part", (i, t)) for t, st in enumerate(parts)]
        for i, (offset, at, proj) in enumerate(wo):
            uses += [(at, "aT", i), (proj, "proj", i)]
        if ffn:
            uses += [(st, "x", k) for k, st in enumerate(X_AT[:ffn])] + [(st, "y", k) for k, st in enumerate(Y_AT[:ffn])]
        uses.sort(key=lambda u: u[0])
        self.uses = [u[1:] for u in uses]
        self.at = {st: [i for i, u in enumerate(uses) if u[0] == st] for st in range(STEPS)}
        fills = sorted([(q[1][0] - 1, "vT", i, q[0]) for i, q in enumerate(qkv)]
                       + [(w[1] - 1, "aT", i, w[0]) for i, w in enumerate(wo)])
        self.nfill = len(fills)
        self.fill = {f[0]: f[1:] for f in fills}
        self.filling = {(kind, i): n for n, (_, kind, i, _) in enumerate(fills)}

    def use(self, kind, n=0):
        return self.uses.index((kind, n))


STAGES = [
    Stage(0, 1, logits=(6, 10, 12), late=20),
    Stage(1, 2, qkv=((1, (2, 3, 4, 5, 6), (12, 14, 15)), (2, (11, 13, 15, 16, 18), (24, 25, 26))), late=27),
    Stage(2, 6, qkv=((2, (2, 4, 6, 10, 13), (19, 21, 24)),), wo=((-2, 28, 30),), ffn=FK, late=26),
    Stage(6, 7, wo=((-2, 28, 30),), ffn=FK_LAST, late=24),
    Stage(7, 8, wo=((-2, 2, 4), (-1, 26, 27))),
]
SPLIT_ACT = {1: "squares", 3: "roots", 5: "first", 7: "second"}
SPLIT_DVE = {2: ("sums",), 4: ("time",), 6: ("rest",), 8: ("last",)}
SPLIT_ALONE = {1: ("squares", "sums"), 2: ("roots",), 4: ("time", "first"), 5: ("rest",), 6: ("second",), 7: ("last",)}
HEAD_HB = 2
HEAD_USES = ([u for hb in range(HEAD_HB) for u in [("vT", hb, 0)] + [("qkv", hb, j) for j in range(HJ)]]
             + [("part", hb, t) for hb in range(HEAD_HB) for t in range(NPART)])
RANK_AT = 17
FIRST_TILES_AT = 22
K_SINH = 11
ADD_AT = ((14, 15, 17, 18), (19, 20, 21, 22), (26, 27, 29, 30))
EPI = ((0, 2 * JT), (2 * JT, 3 * JT), (3 * JT, NT))


def factorial(n):
    return 1.0 if n < 2 else n * factorial(n - 1)


def block_program(nc, x, wqkv, wo, wr, wpack, out):
    assert FT * ST >= TOP * B * S + E * (ST - 1) - ST + 1
    x_d = x.rearrange("b (p j) d -> b p j d", j=JT)
    out_d = out.rearrange("b (p j) d -> b p j d", j=JT)
    qk_d = nc.dram_tensor("qk_parts", (2, B, GB, NPART, DH * HG, S), BF16, kind="Internal").ap()
    v_d = nc.dram_tensor("v_aug", (B, GB, P, JT, HG * VA), F32, kind="Internal").ap()
    xs_d = nc.dram_tensor("expert_in", (FT * ST, D), F32, kind="Internal").ap()
    ys_d = nc.dram_tensor("expert_out", (FT * ST, D), F32, kind="Internal").ap()
    xs_rows = xs_d.rearrange("(f p j) d -> f p j d", p=P, j=SJ)
    ys_rows = ys_d.rearrange("(f p j) d -> f p j d", p=P, j=SJ)

    with ExitStack() as ctx:
        def sb(name, shape, dt=F32):
            return ctx.enter_context(nc.sbuf_tensor(name, shape, dt))

        def sem(name):
            return ctx.enter_context(nc.semaphore(name))

        ps = ctx.enter_context(nc.psum_tensor("ps", [P, 8, 512], F32))

        x_all = sb("x_all", [P, B, JT, D])
        xn_all = sb("xn_all", [P, B, JT, D])
        v_all = sb("v_all", [P, B, JT, D])
        attn = sb("attn", [P, NIT, 2, JT, HG * DH])
        wproj = sb("wproj", [P, NHB, HJ, D])
        osb = sb("osb", [P, QH])[:]
        th = sb("th", [P, 2, ST])[:]
        ga = sb("ga", [P, 2, ST])[:]
        rows4 = sb("rows4", [P, HJ, D])[:]
        rT = sb("rT", [P, QH])[:]
        xs_hi, xs_lo = (sb(n, [P, ST], F32R)[:] for n in ("xs_hi", "xs_lo"))
        w_hi, w_lo = (sb(n, [P, 3, 2, P], F32R)[:] for n in ("w_hi", "w_lo"))
        stats = sb("stats", [P, JT, 6])
        mv = sb("mv", [P, NT, 2])
        ident = sb("ident", [P, P])
        identb = sb("identb", [P, P], BF16)
        wqkv_s = sb("wqkv_s", [P, 3 * D])
        wo_s = sb("wo_s", [P, D])
        wr_s = sb("wr_s", [P, E])
        col = {n: sb("c_" + n, [P, B, JT]) for n in (
            "sd", "rstd", "ss", "x0", "z", "zp", "m", "r", "a", "ln", "d", "d0", "dd", "q", "dn",
            "dne", "rec", "sc", "v0", "w1", "w2")}
        slot = [sb(f"slot{k}", [P, NT], U32) for k in range(TOP)]
        tile_expert = sb("tile_expert", [1, FT], I32)
        qk = sb("qk", [P, HJ, 2 * D])
        rest = sb("rest", [P, HJ, 2 * D])
        qss = sb("qss", [P, 2 * HJ * GB, HG])
        parts = sb("parts", [P, NPART, HJ, 2 * D], BF16)
        partT = sb("partT", [P, NPART, 2, HJ * P], BF16)
        vbuf = sb("vbuf", [P, GB, HJ, HG * VA])
        qst = [sb(f"qst{k}", [KROWS, HG, S], BF16) for k in range(2)]
        kst = [sb(f"kst{k}", [KROWS, HG, S], BF16) for k in range(2)]
        vst = [sb(f"vst{k}", [P, JT, HG * VA]) for k in range(2)]
        ex = sb("ex", [P, 2, HG, QH])
        orec = sb("orec", [P, HJ, HG])
        w_ex = [sb(f"w_ex{k}", [P, WCOL]) for k in range(TB)]
        xs_s = [sb(f"xs_s{k}", [P, SJ, D]) for k in range(TB)]
        ys_s = [sb(f"ys_s{k}", [P, SJ, D]) for k in range(YB)]
        hT = sb("hT", [P, 2, 3, ST])
        tiny = {n: sb("t_" + n, [P, NT]) for n in ("m1", "m2", "r1", "r2", "dm", "em", "s1")}
        iota_e = sb("iota_e", [P, E])
        iota_n = sb("iota_n", [P, B * S // ST])
        iota_t = sb("iota_t", [1, FT])
        cnt = {n: sb("n_" + n, [P, E]) for n in ("n", "tl", "ct", "off")}




        qk_1, rest_1 = (w_ex[i][:, 0:HJ * 2 * D].rearrange("p (j n) -> p j n", j=HJ) for i in range(2))
        partT_1 = ex[:].rearrange("p a h q -> p (a h q)").bitcast(BF16)[:, 0:NPART * 2 * HJ * P].rearrange(
            "p (t w s) -> p t w s", t=NPART, w=2)
        vsq = w_ex[0][:, 0:S].rearrange("p (j d) -> p j d", d=D)
        xnT, zeros = w_ex[1][:, 0:S], w_ex[2][:, 0:1024]
        tri, ones, one8 = w_ex[3][:, 0:P], w_ex[3][:, P:2 * P], w_ex[3][:, 2 * P:2 * P + E * NT]
        rt = {n: wproj[:].rearrange("p a j d -> p (a j d)")[:, 256 * i:256 * (i + 1)] for i, n in enumerate(
            ("logit", "eq", "oh1", "l2", "oh2", "mask", "tot", "incl", "excl", "rk", "s1p", "cmp", "tail"))}
        te = lambda n: rt[n].rearrange("p (t e) -> p t e", e=E)
        et = lambda n: rt[n].rearrange("p (e t) -> p e t", e=E)
        ni = iota_n.shape[1]
        esq = rest[:].rearrange("p j n -> p (j n)").rearrange("p (t d) -> p t d", d=D)
        cmp16 = rt["cmp"][:, 0:E * ni].rearrange("p (e i) -> p e i", e=E)
        rest_r = wproj[:].rearrange("p a j d -> p (a j d)")[0:1, 3328:]
        cmpt = rest_r[:, 0:FT * E].rearrange("p (f e) -> p f e", e=E)
        tef = rest_r[:, FT * E:FT * E + FT]

        def bank(n, dt=F32):
            return ps[:, n, :] if dt == F32 else ps[:, n, :].bitcast(dt)

        O_BANK, GU_BANK, LENT = 4, 5, 7

        names = """consts x_loaded w_loaded zeros_set zero_filled vbuf_ones stacks_zero
            stats_ready mv_ready sd_ready rstd_ready xn_ready clipped vsq_ready ss_ready
            xnT_psum xnT_ready head_logits logits_read
            chain_dve chain_roots ln_ready root_dve router_dve mask_ready rank_psum exp_dm slots_ready experts_ready
            scattered
            rows_ready lent_written lent_read qksq_ready qkss_ready q0_ready comp0
            p0_ready rest_ready p1_ready p2_ready part_stored v_stored
            scores_ready exp_done pv_done o_free o_rec
            xs_hi_ready w_hi_ready w_split gu_psum tanh_done gate_done h_ready
            norm2_ready norm_ready epi_dve fss_ready x0_ready y_added out_ready out_stored""".split()
        s = {n: sem(n) for n in names}
        stack_loaded = [sem(f"stack_loaded{k}") for k in range(2)]
        tile_loaded = [sem(f"tile_loaded{k}") for k in range(TB)]
        y_stored = [sem(f"y_stored{k}") for k in range(YB)]
        y_back = [sem(f"y_back{b}") for b in range(B)]
        NZERO = -(-FT * ST * D // P // 1024)
        NSTACK = 1 + NPART + 1

        def affine(i, a, c):
            return i * a + c

        def lent_base(sg, it):
            before = len(HEAD_USES) + sum(len(t.uses) * (t.hi - t.lo) for t in STAGES if t.hi <= sg.lo)
            return lambda c: affine(it, len(sg.uses), before - sg.lo * len(sg.uses) + c)

        def rows_base(sg, it):
            before = HEAD_HB + sum(t.nfill * (t.hi - t.lo) for t in STAGES if t.hi <= sg.lo)
            return lambda c: affine(it, sg.nfill, before - sg.lo * sg.nfill + c)

        LENT_ALL = len(HEAD_USES) + sum(len(t.uses) * (t.hi - t.lo) for t in STAGES)
        ROWS_ALL = HEAD_HB + sum(t.nfill * (t.hi - t.lo) for t in STAGES)

        def run(eng, body):
            for sg in STAGES:
                if sg.hi - sg.lo == 1:
                    body(sg, sg.lo)
                else:
                    with eng.Fori(sg.lo, sg.hi) as it:
                        body(sg, it)

        block = ctx.enter_context(nc.Block())

        @block.sync
        def _(sp):
            for k in range(YB):
                sp.sem_inc(y_stored[k], 16)
            sp.dma_start(x_all[:, 0], x_d[0]).then_inc(s["x_loaded"], 16)
            sp.dma_start(wqkv_s[:], wqkv).then_inc(s["w_loaded"], 16)
            sp.dma_start(wr_s[:], wr).then_inc(s["w_loaded"], 16)
            sp.dma_start(wo_s[:], wo).then_inc(s["w_loaded"], 16)
            for b in range(1, B):
                sp.wait_ge(s["x_loaded"], 16 * b)
                sp.dma_start(x_all[:, b], x_d[b]).then_inc(s["x_loaded"], 16)

            def store_v(b, half):
                sp.dma_start(v_d.rearrange("b g p (a j) n -> b a p g (j n)", a=2)[b, half],
                             vbuf[:].rearrange("p g j n -> p g (j n)")).then_inc(s["v_stored"], 16)

            def store_part(b, half, t, src=partT):
                dst = qk_d.rearrange("w b g t n (a s) -> w b t a g n s", a=2)
                for w in range(2):
                    sp.dma_start(dst[w, b, t, half], src[:, t, w, :]).then_inc(s["part_stored"], 16)

            def load_stack(g, par):
                k_rows = qk_d.rearrange("w b g t n s -> w (b g) (t n) s").rearrange("w g (tc h) s -> w g tc (h s)", h=HG)
                q_rows = qk_d.rearrange("w b g t (c h) s -> w (b g) t c (h s)", h=HG)
                sp.dma_start(kst[par][0:SROWS].rearrange("r h s -> r (h s)"),
                             k_rows[1, bass.ds(g, 1)].to_broadcast((NPART, NPART * DH, HG * S))
                             ).then_inc(stack_loaded[par], 16)
                for r in range(NPART):
                    rows = slice(NPART * DH * r, NPART * DH * (r + 1))
                    sp.dma_start(qst[par][rows].rearrange("r h s -> r (h s)"),
                                 q_rows[0, g, r:r + 1].to_broadcast((NPART, DH, HG * S))
                                 ).then_inc(stack_loaded[par], 16)
                sp.dma_start(vst[par][:].rearrange("p j n -> p (j n)"),
                             v_d.rearrange("b g p j n -> (b g) p (j n)")[g]).then_inc(stack_loaded[par], 16)

            def load_tile(f, k):
                e = sp.value_load(tile_expert[0:1, bass.ds(f, 1)], min_val=0, max_val=E - 1)
                sp.dma_start(w_ex[k][:], wpack[e]).then_inc(tile_loaded[k], 16)
                sp.dma_start(xs_s[k][:], xs_rows[f]).then_inc(tile_loaded[k], 16)

            for u, (kind, hb, n) in enumerate(HEAD_USES):
                if (kind, n) == ("qkv", HJ - 1):
                    sp.wait_ge(s["lent_read"], u + 1)
                    store_v(hb // 2, hb % 2)
                elif kind == "part":
                    sp.wait_ge(s["lent_read"], u + 1)
                    store_part(hb // 2, hb % 2, n, (partT, partT_1)[hb])
            sp.wait_ge(s["part_stored"], 16 * 2 * NPART * HEAD_HB)
            sp.wait_ge(s["v_stored"], 16 * HEAD_HB)
            sp.wait_ge(s["stacks_zero"], 4)
            load_stack(0, 0)
            load_stack(1, 1)
            sp.wait_ge(s["zeros_set"], 1)
            flat = xs_d.rearrange("(p r) d -> p (r d)", p=P)
            for i in range(NZERO):
                part = flat[:, 1024 * i:min(1024 * (i + 1), flat.shape[1])]
                sp.dma_start(part, zeros[:, 0:part.shape[1]]).then_inc(s["zero_filled"], 16)

            def iteration(sg, it):
                lent = lent_base(sg, it)
                for st in range(STEPS):
                    if st == 1 and sg.carry:
                        sp.wait_ge(s["pv_done"], it * 4)
                        load_stack(it * 2 + 1, 1)
                    if st in sg.y_at:
                        k = sg.y_at.index(st)
                        sp.wait_ge(s["lent_read"], lent(sg.use("y", k) + 1))
                        f = affine(it, FK, k - FFN0 * FK)
                        sp.dma_start(ys_rows[f], ys_s[k % YB][:]).then_inc(y_stored[k % YB], 16)
                        if sg.hi < FFN0 + NFFN or k < sg.ffn - TB:
                            load_tile(affine(it, FK, k - FFN0 * FK + TB), k % TB)
                    if sg.hi == FFN0 and st == FIRST_TILES_AT:
                        sp.wait_ge(s["experts_ready"], 1)
                        sp.wait_ge(s["scattered"], 16 * TOP * NT)
                        for k in range(TB):
                            load_tile(k, k)
                    for i, (offset, steps, parts_at) in enumerate(sg.qkv):
                        hb = it + offset
                        if st == steps[-1]:
                            sp.wait_ge(s["lent_read"], lent(sg.use("qkv", (i, HJ - 1)) + 1))
                            store_v(hb // 2, hb % 2)
                        if st in parts_at:
                            t = parts_at.index(st)
                            sp.wait_ge(s["lent_read"], lent(sg.use("part", (i, t)) + 1))
                            store_part(hb // 2, hb % 2, t)
                    if st == sg.late:
                        sp.wait_ge(s["pv_done"], it * 4 + 2)
                        if sg.qkv:
                            sp.wait_ge(s["part_stored"], affine(it, 32 * NPART, 3 * 32 * NPART))
                            sp.wait_ge(s["v_stored"], affine(it, 16, 3 * 16))
                        load_stack(it * 2 + 2, 0)

            run(sp, iteration)
            for b in range(B):
                sp.wait_ge(s["out_ready"], b + 1)
                sp.dma_start(out_d[b], x_all[:, b]).then_inc(s["out_stored"], 16)
            sp.wait_ge(s["out_stored"], 16 * B)

        @block.gpsimd
        def _(pool):
            g = nc.gpsimd
            c = s["consts"]
            g.memset(ident[:], 0.0).then_inc(c, 1)
            g.memset(identb[:], 0.0).then_inc(c, 1)
            g.memset(tri[:], 1.0).then_inc(c, 1)
            g.memset(ones[:], 1.0).then_inc(c, 1)
            g.memset(one8[:], 1.0).then_inc(c, 1)
            pool.wait_ge(c, 5)
            eye = dict(compare_op=ALU.not_equal, fill=1.0, base=0, pattern=[[-1, P]], channel_multiplier=1)
            g.affine_select(out=ident[:], in_=ident[:], **eye).then_inc(c, 1)
            g.affine_select(out=identb[:], in_=identb[:], **eye).then_inc(c, 1)
            g.affine_select(out=tri[:], in_=tri[:], compare_op=ALU.is_gt, fill=0.0, base=0, pattern=[[1, P]],
                            channel_multiplier=-1).then_inc(c, 1)
            g.iota(iota_e[:], [[-1, E]], base=E, channel_multiplier=0,
                   allow_small_or_imprecise_dtypes=True).then_inc(c, 1)
            g.iota(iota_n[:], [[ST, iota_n.shape[1]]], base=0, channel_multiplier=0,
                   allow_small_or_imprecise_dtypes=True).then_inc(c, 1)
            g.iota(iota_t[:], [[1, FT]], base=0, channel_multiplier=0,
                   allow_small_or_imprecise_dtypes=True).then_inc(c, 1)
            g.memset(vbuf[:], 1.0).then_inc(s["vbuf_ones"], 1)
            pool.wait_ge(s["vbuf_ones"], 1)
            for i, stack in enumerate((kst[0], qst[0], kst[1], qst[1])):
                g.memset(stack[64:KROWS], 0.0).then_inc(s["stacks_zero"], 1)
                pool.wait_ge(s["stacks_zero"], i + 1)
            g.memset(zeros, 0.0).then_inc(s["zeros_set"], 1)

            for b in range(1, B):
                pool.wait_ge(s["clipped"], b + 1)
                pool.wait_ge(s["ss_ready"], b)
                v = v_all[:, b, :, 1:]
                g.tensor_tensor(vsq[:, :, 1:], v, v, ALU.mult).then_inc(s["vsq_ready"], 1)
            pool.wait_ge(s["slots_ready"], TOP)
            pool.wait_ge(s["zero_filled"], 16 * NZERO)
            rows = xn_all[:].rearrange("p b j d -> p (b j) d")
            for t in range(NT):
                for k in range(TOP):
                    g.indirect_dma_start(xs_d, bass.IndirectOffsetOnAxis(ap=slot[k][:, t:t + 1], axis=0),
                                         rows[:, t, :], None).then_inc(s["scattered"], 16)

            for k in range(YB):
                pool.wait_ge(y_stored[k], 16 + 16 * len(range(k, FT, YB)))
            pool.wait_ge(s["scattered"], 16 * TOP * NT)
            for t in range(NT):
                for k, dst in ((0, xn_all), (1, v_all)):
                    g.indirect_dma_start(dst[:].rearrange("p b j d -> p (b j) d")[:, t, :], None, ys_d,
                                         bass.IndirectOffsetOnAxis(ap=slot[k][:, t:t + 1], axis=0)
                                         ).then_inc(y_back[t // JT], 16)

        @block.scalar
        def _(act):
            A = nc.scalar.activation

            def number(n, t0, t1):
                return col[n][:].rearrange("p b j -> p (b j)")[:, t0:t1]

            def deviation(t0, t1):
                act.wait_ge(s["mv_ready"], t1 // JT)
                A(number("sd", t0, t1), mv[:, t0:t1, 1], ACT.Sqrt, bias=LN_EPS).then_inc(s["sd_ready"], 1)

            def log_map(part, group, t0, t1):
                if part == "x0":
                    act.wait_ge(s["ss_ready"], t1 // JT)
                    A(number("x0", t0, t1), number("ss", t0, t1), ACT.Sqrt, bias=1.0 + EPS).then_inc(s["chain_roots"], 1)
                elif part == "roots":
                    act.wait_ge(s["chain_dve"], 13 * group + 3)
                    A(number("r", t0, t1), number("m", t0, t1), ACT.Sqrt).then_inc(s["chain_roots"], 1)
                    act.wait_ge(s["chain_dve"], 13 * group + 7)
                    A(number("dn", t0, t1), number("q", t0, t1), ACT.Sqrt).then_inc(s["chain_roots"], 1)
                else:
                    act.wait_ge(s["chain_dve"], 13 * group + 8)
                    A(number("ln", t0, t1), number("a", t0, t1), ACT.Ln).then_inc(s["ln_ready"], 1)

            deviation(0, JT)
            act.wait_ge(s["clipped"], 1)
            A(vsq[:, :, 1:], v_all[:, 0, :, 1:], ACT.Square).then_inc(s["vsq_ready"], 1)
            for part in ("x0", "roots", "log"):
                log_map(part, 0, 0, JT)

            def split(part, hb, qk=qk, rest=rest):
                if part == "squares":
                    A(rest[:], qk[:], ACT.Square).then_inc(s["qksq_ready"], 1)
                elif part == "roots":
                    act.wait_ge(s["qkss_ready"], hb + 1)
                    A(qss[:], qss[:], ACT.Sqrt, bias=1.0 + EPS).then_inc(s["q0_ready"], 1)
                elif part == "first":
                    act.wait_ge(s["comp0"], affine(hb, 2, 2))
                    A(parts[:, 0], qk[:], ACT.Copy).then_inc(s["p0_ready"], 1)
                else:
                    act.wait_ge(s["rest_ready"], hb + 1)
                    A(parts[:, 1], rest[:], ACT.Copy).then_inc(s["p1_ready"], 1)

            for part, hb in (("squares", 0), ("roots", 0), ("first", 0), ("squares", 1), ("second", 0), ("roots", 1),
                             ("first", 1), ("second", 1)):
                if part == "squares":
                    act.wait_ge(s["lent_read"], HEAD_USES.index(("qkv", hb, HJ - 1)) + 1)
                split(part, hb, (qk, qk_1)[hb], (rest, rest_1)[hb])

            def iteration(sg, it):
                for st in range(STEPS):
                    if st - 1 in sg.gu:
                        n = sg.gu[st - 1]
                        m = IC[n % 3][1]
                        act.wait_ge(s["gu_psum"], affine(it, GU, n + 1 - FFN0 * GU))
                        A(th[0:m, n % 2, :], bank(GU_BANK + n % 2)[0:m, 0:ST], ACT.Tanh,
                          scale=0.5).then_inc(s["tanh_done"], 1)
                    for hp in range(2):
                        act.wait_ge(s["scores_ready"], affine(it, 2 * STEPS, 2 * st + hp + 1))
                        A(ex[:, st % 2, 2 * hp:2 * hp + 2, :], ps[:, 2 * hp:2 * hp + 2, :], ACT.Exp,
                          scale=DH ** -0.5, bias=SHIFT).then_inc(s["exp_done"], 1)
                    for i, (offset, steps, _) in enumerate(sg.qkv if sg.ffn else ()):
                        if st == steps[-1] + 1:
                            act.wait_ge(s["lent_read"], lent_base(sg, it)(sg.use("qkv", (i, HJ - 1)) + 1))
                        if st - steps[-1] in SPLIT_ACT:
                            split(SPLIT_ACT[st - steps[-1]], it + offset)
                    if sg.lo == 0:
                        if st == 24:
                            log_map("log", 1, JT, NT)
                        if st == 19:
                            act.wait_ge(s["mask_ready"], 2)
                            A(tiny["em"][:], tiny["dm"][:], ACT.Exp).then_inc(s["exp_dm"], 1)
                    if sg.lo == NIT - 2:
                        if st == 8:
                            norms(0)
                        if st == 19:
                            time_parts(0, 1)

            def norms(group):
                act.wait_ge(s["norm2_ready"], group + 1)
                A(number("sd", *EPI[group]), number("q", *EPI[group]), ACT.Sqrt).then_inc(s["norm_ready"], 1)

            def time_parts(group, count):
                act.wait_ge(s["fss_ready"], count)
                A(number("x0", *EPI[group]), number("ss", *EPI[group]), ACT.Sqrt, bias=1.0 + EPS
                  ).then_inc(s["x0_ready"], 1)

            run(act, iteration)
            norms(2)
            time_parts(2, 2)

        @block.vector
        def _(dve):
            V = nc.vector

            tiles = lambda v: v.rearrange("p b j d -> p (b j) d")
            number = lambda n: col[n][:].rearrange("p b j -> p (b j)")

            root_steps = [0]

            def root(out, x, tmp, plus=0.0):
                n = x.shape[1]
                xs, y, r = (tmp[:, i * n:(i + 1) * n] for i in range(3))

                def step(ins):
                    root_steps[0] += 1
                    ins.then_inc(s["root_dve"], 1)
                    dve.wait_ge(s["root_dve"], root_steps[0])

                step(V.tensor_scalar(xs, x, plus, None, ALU.add))
                step(V.tensor_scalar(y.bitcast(I32), xs.bitcast(I32), 1, None, ALU.logical_shift_right))
                step(V.tensor_scalar(y.bitcast(I32), y.bitcast(I32), float(0x1FBD1DF5), None, ALU.add))
                for i in range(3):
                    step(V.reciprocal(r, y))
                    step(V.scalar_tensor_tensor(out=r, in0=r, scalar=0.5, in1=xs, op0=ALU.mult, op1=ALU.mult))
                    if i < 2:
                        step(V.scalar_tensor_tensor(out=y, in0=y, scalar=0.5, in1=r, op0=ALU.mult, op1=ALU.add))
                return V.scalar_tensor_tensor(out=out, in0=y, scalar=0.5, in1=r, op0=ALU.mult, op1=ALU.add)

            root_tmp_0 = w_ex[3][:, 512:1024]
            root_tmp = wproj[:, NHB - 1].rearrange("p j d -> p (j d)")

            def token_stats(b):
                dve.wait_ge(s["x_loaded"], 16 * (b + 1))
                if b:
                    dve.wait_ge(s["mv_ready"], b)
                for j in range(JT):
                    ins = V.bn_stats(stats[:, j], x_all[:, b, j])
                ins.then_inc(s["stats_ready"], 1)
                dve.wait_ge(s["stats_ready"], b + 1)
                for j in range(JT):
                    ins = V.bn_aggr(mv[:, b * JT + j], stats[:, j])
                ins.then_inc(s["mv_ready"], 1)

            def inverse_deviation(group, t0, t1):
                dve.wait_ge(s["sd_ready"], group + 1)
                V.reciprocal(number("rstd")[:, t0:t1], number("sd")[:, t0:t1]).then_inc(s["rstd_ready"], 1)
                dve.wait_ge(s["rstd_ready"], group + 1)

            def normalise(b):
                for t in range(b * JT, (b + 1) * JT):
                    ins = V.tensor_scalar(tiles(xn_all[:])[:, t], tiles(x_all[:])[:, t], mv[:, t, 0:1],
                                          number("rstd")[:, t:t + 1], ALU.subtract, ALU.mult)
                ins.then_inc(s["xn_ready"], 1)
                dve.wait_ge(s["xn_ready"], b + 1)
                V.tensor_scalar(v_all[:, b], xn_all[:, b], 8.0, -8.0, ALU.min, ALU.max).then_inc(s["clipped"], 1)

            def turn_xn(b):
                if b:
                    dve.wait_ge(s["logits_read"], b)
                for half in range(2):
                    dve.wait_ge(s["xnT_psum"], 2 * b + half + 1)
                    V.tensor_copy(xnT[:, half * QH:(half + 1) * QH], bank(GU_BANK + half)).then_inc(s["xnT_ready"], 1)

            def keep_logits(b, src):
                return V.tensor_copy(rt["logit"][:, b * JT * E:(b + 1) * JT * E], src[:, 0:JT * E]
                                     ).then_inc(s["logits_read"], 1)

            def sum_v(b):
                dve.wait_ge(s["vsq_ready"], b + 1)
                V.tensor_reduce(col["ss"][:, b], vsq[:, :, 1:], AX.X, ALU.add).then_inc(s["ss_ready"], 1)

            done = [0]

            def link(ins):
                done[0] += 1
                ins.then_inc(s["chain_dve"], 1)
                dve.wait_ge(s["chain_dve"], done[0])

            def log_map(part, group, t0, t1):
                C = {n: number(n)[:, t0:t1] for n in col}
                if part == "first":
                    dve.wait_ge(s["chain_roots"], 3 * group + 1)
                    link(V.tensor_scalar(C["z"], C["x0"], 1.0 + EPS, None, ALU.max))
                    link(V.tensor_scalar(C["zp"], C["z"], 1.0, None, ALU.add))
                    link(V.scalar_tensor_tensor(out=C["m"], in0=C["z"], scalar=-1.0, in1=C["zp"], op0=ALU.add,
                                                op1=ALU.mult))
                    link(V.tensor_tensor(C["d0"], C["x0"], C["z"], ALU.subtract))
                    link(V.tensor_tensor(C["dd"], C["d0"], C["d0"], ALU.mult))
                    link(V.tensor_tensor(C["dne"], C["ss"], C["dd"], ALU.subtract))
                    link(V.tensor_scalar(C["q"], C["dne"], EPS, None, ALU.max))
                elif part == "second":
                    dve.wait_ge(s["chain_roots"], 3 * group + 2)
                    link(V.tensor_tensor(C["a"], C["z"], C["r"], ALU.add))
                    dve.wait_ge(s["chain_roots"], 3 * group + 3)
                    link(V.tensor_scalar(C["dne"], C["dn"], EPS, None, ALU.add))
                    link(V.reciprocal(C["rec"], C["dne"]))
                else:
                    dve.wait_ge(s["ln_ready"], group + 1)
                    link(V.tensor_scalar(C["d"], C["ln"], 1e-3, None, ALU.max))
                    link(V.tensor_tensor(C["sc"], C["d"], C["rec"], ALU.mult))
                    link(V.tensor_tensor(C["v0"], C["sc"], C["d0"], ALU.mult))

            token_stats(0)
            inverse_deviation(0, 0, JT)
            normalise(0)
            turn_xn(0)
            sum_v(0)
            for part in ("first", "second", "third"):
                log_map(part, 0, 0, JT)
            dve.wait_ge(s["head_logits"], 1)
            keep_logits(0, bank(0))

            def fill_v(hb):
                t = bass.ds(hb * HJ, HJ)
                V.tensor_tensor(rows4[:, :, 1:], tiles(v_all[:])[:, t, 1:],
                                number("sc")[:, t].unsqueeze(2).to_broadcast((P, HJ, D - 1)), ALU.mult)
                V.tensor_copy(rows4[:, :, 0], number("v0")[:, t]).then_inc(s["rows_ready"], 1)

            def read_qkv(src, j, qk=qk):
                V.tensor_scalar(qk[:, j, :], src[:, 0:2 * D], QKCLIP, -QKCLIP, ALU.min, ALU.max)
                V.tensor_copy(vbuf[:, :, j, :].rearrange("p g (h c) -> p g h c", h=HG)[:, :, :, 0:DH],
                              src[:, 2 * D:3 * D].rearrange("p (g h c) -> p g h c", g=GB, h=HG)
                              ).then_inc(s["lent_read"], 1)

            tq = qss[:].rearrange("p (j w g) h -> p j w g h", j=HJ, w=2)

            def split(part, hb, qk=qk, rest=rest):
                wgc = qk[:].rearrange("p j (w g c h) -> p j w g c h", w=2, g=GB, c=DH)
                sums = rest[:].rearrange("p j n -> p (j n)").rearrange("p (n c h) -> p n h c", c=DH, h=HG)[:, :, :, 1:]
                if part == "squares":
                    dve.wait_ge(s["lent_read"], lent_base(STAGES[1], 1)(STAGES[1].use("qkv", (hb - 2, HJ - 1)) + 1))
                    V.tensor_tensor(rest[:], qk[:], qk[:], ALU.mult).then_inc(s["qksq_ready"], 1)
                elif part == "roots":
                    q_and_k = qss[:].rearrange("p n h -> p (n h)")
                    dve.wait_ge(s["qkss_ready"], hb + 1)
                    root(q_and_k, q_and_k, root_tmp, 1.0 + EPS).then_inc(s["q0_ready"], 1)
                elif part == "first":
                    dve.wait_ge(s["comp0"], affine(hb, 2, 2))
                    V.tensor_copy(parts[:, 0], qk[:]).then_inc(s["p0_ready"], 1)
                elif part == "second":
                    dve.wait_ge(s["rest_ready"], hb + 1)
                    V.tensor_copy(parts[:, 1], rest[:]).then_inc(s["p1_ready"], 1)
                elif part == "sums":
                    dve.wait_ge(s["qksq_ready"], hb + 1)
                    V.tensor_reduce(qss[:], sums, AX.X, ALU.add).then_inc(s["qkss_ready"], 1)
                elif part == "time":
                    dve.wait_ge(s["q0_ready"], hb + 1)
                    V.tensor_scalar(wgc[:, :, 0, :, 0, :], tq[:, :, 0], -1.0, None, ALU.mult).then_inc(s["comp0"], 1)
                    V.tensor_copy(wgc[:, :, 1, :, 0, :], tq[:, :, 1]).then_inc(s["comp0"], 1)
                elif part == "rest":
                    dve.wait_ge(s["p0_ready"], hb + 1)
                    V.tensor_tensor(rest[:], qk[:], parts[:, 0], ALU.subtract).then_inc(s["rest_ready"], 1)
                else:
                    dve.wait_ge(s["p1_ready"], hb + 1)
                    V.tensor_tensor(parts[:, 2], rest[:], parts[:, 1], ALU.subtract).then_inc(s["p2_ready"], 1)

            def part_copy(src, t, partT=partT):
                V.tensor_copy(partT[:, t].rearrange("p w s -> p (w s)"), src).then_inc(s["lent_read"], 1)

            dve.wait_ge(s["vbuf_ones"], 1)
            def head_use(kind, hb, n):
                u = HEAD_USES.index((kind, hb, n))
                dve.wait_ge(s["lent_written"], u + 1)
                src = O_BANK + u % 4
                if kind == "vT":
                    V.tensor_copy(rT, bank(src)).then_inc(s["lent_read"], 1)
                elif kind == "qkv":
                    if n == 0 and hb:
                        dve.wait_ge(s["v_stored"], 16 * hb)
                    read_qkv(bank(src), n, (qk, qk_1)[hb])
                else:
                    part_copy(bank(src, BF16), n, (partT, partT_1)[hb])

            fill_v(0)
            head_use("vT", 0, 0)
            for j in range(HJ):
                head_use("qkv", 0, j)
            fill_v(1)
            split("sums", 0)
            head_use("vT", 1, 0)
            split("time", 0)
            for j in range(HJ):
                head_use("qkv", 1, j)
            split("rest", 0)
            head_use("part", 0, 0)
            split("sums", 1, qk_1, rest_1)
            split("last", 0)
            head_use("part", 0, 1)
            split("time", 1, qk_1, rest_1)
            head_use("part", 0, 2)
            split("rest", 1, qk_1, rest_1)
            head_use("part", 1, 0)
            split("last", 1, qk_1, rest_1)
            head_use("part", 1, 1)
            head_use("part", 1, 2)

            dve.wait_ge(s["lent_read"], len(HEAD_USES))
            V.memset(bank(O_BANK), 0.0).then_inc(s["o_free"], 1)

            steps = [0]

            def R(ins):
                steps[0] += 1
                ins.then_inc(s["router_dve"], 1)
                dve.wait_ge(s["router_dve"], steps[0])

            by_e = lambda v: v.unsqueeze(2).to_broadcast((P, NT, E))
            by_t = lambda v: v.unsqueeze(2).to_broadcast((P, E, NT))
            iota_te = iota_e[:].unsqueeze(1).to_broadcast((P, NT, E))
            T = {n: t[:] for n, t in tiny.items()}
            N = {n: t[:] for n, t in cnt.items()}

            def best_expert(best, oh, key, src):
                R(V.tensor_reduce(T[best], te(src), AX.X, ALU.max))
                R(V.tensor_tensor(te("eq"), te(src), by_e(T[best]), ALU.is_equal))
                R(V.tensor_tensor(te("eq"), te("eq"), iota_te, ALU.mult))
                R(V.tensor_reduce(T[key], te("eq"), AX.X, ALU.max))
                R(V.tensor_tensor(te(oh), iota_te, by_e(T[key]), ALU.is_equal))

            def choose_first():
                dve.wait_ge(s["logits_read"], B)
                dve.wait_ge(s["consts"], 11)
                best_expert("m1", "oh1", "r1", "logit")

            def choose_second():
                R(V.scalar_tensor_tensor(out=rt["l2"], in0=rt["oh1"], scalar=-BIG, in1=rt["logit"], op0=ALU.mult,
                                         op1=ALU.add))
                best_expert("m2", "oh2", "r2", "l2")

            def choices():
                V.tensor_tensor(et("mask").rearrange("p e t -> p t e"), te("oh1"), te("oh2"), ALU.add
                                ).then_inc(s["mask_ready"], 1)
                V.tensor_tensor(T["dm"], T["m2"], T["m1"], ALU.subtract).then_inc(s["mask_ready"], 1)

            def counts():
                dve.wait_ge(s["rank_psum"], 1)
                R(V.tensor_copy(rt["tot"], bank(GU_BANK)[:, 0:E * NT]))
                R(V.tensor_tensor_scan(rt["incl"], one8[:], rt["tot"], 0.0, ALU.mult, ALU.add))
                R(V.tensor_tensor(rt["excl"], rt["incl"], rt["tot"], ALU.subtract))

            def expert_offsets():
                R(V.tensor_tensor(N["n"], et("incl")[:, :, NT - 1], et("excl")[:, :, 0], ALU.subtract))
                R(V.tensor_tensor(cmp16, N["n"].unsqueeze(2).to_broadcast((P, E, ni)),
                                  iota_n[:].unsqueeze(1).to_broadcast((P, E, ni)), ALU.is_gt))
                R(V.tensor_reduce(N["tl"], cmp16, AX.X, ALU.add))
                R(V.tensor_tensor_scan(N["ct"], one8[:, 0:E], N["tl"], 0.0, ALU.mult, ALU.add))
                R(V.tensor_tensor(N["off"], N["ct"], N["tl"], ALU.subtract))
                R(V.scalar_tensor_tensor(out=N["off"], in0=N["off"], scalar=float(ST), in1=et("excl")[:, :, 0],
                                         op0=ALU.mult, op1=ALU.subtract))

            def ranks():
                R(V.tensor_tensor(et("excl"), et("excl"), by_t(N["off"]), ALU.add))
                R(V.tensor_tensor(rt["rk"], rt["excl"], bank(GU_BANK)[:, E * NT:2 * E * NT], ALU.add))

            def slots(k, oh):
                R(V.tensor_tensor(te("s1p"), te(oh), et("rk").rearrange("p e t -> p t e"), ALU.mult))
                R(V.tensor_reduce(T["s1"], te("s1p"), AX.X, ALU.add))
                V.tensor_copy(slot[k][:], T["s1"]).then_inc(s["slots_ready"], 1)
                dve.wait_ge(s["slots_ready"], k + 1)

            def tile_experts():
                R(V.tensor_tensor(cmpt, iota_t[:].unsqueeze(2).to_broadcast((1, FT, E)),
                                  N["ct"][0:1].unsqueeze(1).to_broadcast((1, FT, E)), ALU.is_ge))
                R(V.tensor_reduce(tef, cmpt, AX.X, ALU.add))
                V.tensor_scalar(tile_expert[:], tef, float(E - 1), None, ALU.min).then_inc(s["experts_ready"], 1)

            def expert_weights():
                dve.wait_ge(s["exp_dm"], 1)
                R(V.tensor_scalar(T["s1"], T["em"], 1.0, None, ALU.add))
                R(V.reciprocal(number("w1"), T["s1"]))
                R(V.tensor_tensor(number("w2"), T["em"], number("w1"), ALU.mult))

            def first_iteration_step(st):
                if st < 3:
                    token_stats(1 + st)
                if st == 3:
                    dve.wait_ge(s["mv_ready"], B)
                    root(number("sd")[:, JT:NT], mv[:, JT:NT, 1], root_tmp_0, LN_EPS).then_inc(s["sd_ready"], 1)
                if st == 4:
                    inverse_deviation(1, JT, NT)
                if st in (4, 5, 6):
                    normalise(st - 3)
                if st in STAGES[0].logits:
                    turn_xn(1 + STAGES[0].logits.index(st))
                if st in (7, 10, 12):
                    sum_v({7: 1, 10: 2, 12: 3}[st])
                if st == 19:
                    dve.wait_ge(s["ss_ready"], B)
                if st in (19, 21, 22):
                    out, x, plus = {19: ("x0", "ss", 1.0 + EPS), 21: ("r", "m", 0.0), 22: ("dn", "q", 0.0)}[st]
                    root(number(out)[:, JT:NT], number(x)[:, JT:NT], root_tmp_0, plus).then_inc(s["chain_roots"], 1)
                if st in (20, 22, 27):
                    log_map({20: "first", 22: "second", 27: "third"}[st], 1, JT, NT)
                if st == 13:
                    choose_first()
                if st == 14:
                    choose_second()
                if st == 15:
                    choices()
                if st == RANK_AT:
                    counts()
                    expert_offsets()
                    ranks()
                if st == RANK_AT + 1:
                    slots(0, "oh1")
                    slots(1, "oh2")
                if st == RANK_AT + 8:
                    tile_experts()
                    expert_weights()

            wp, xt, y1, y2 = wproj[:].rearrange("p a j d -> p (a j) d"), tiles(x_all[:]), tiles(xn_all[:]), tiles(v_all[:])
            links = [0]

            def L(ins):
                links[0] += 1
                ins.then_inc(s["epi_dve"], 1)
                dve.wait_ge(s["epi_dve"], links[0])

            def sum_squares(t0, t1):
                L(V.tensor_tensor(esq[:, 0:t1 - t0, 1:], wp[:, t0:t1, 1:], wp[:, t0:t1, 1:], ALU.mult))
                L(V.tensor_reduce(number("ss")[:, t0:t1], esq[:, 0:t1 - t0, 1:], AX.X, ALU.add))

            def norm_squares(group):
                t0, t1 = EPI[group]
                V.tensor_scalar(number("q")[:, t0:t1], number("ss")[:, t0:t1], 0.0, EPS, ALU.max, ALU.add
                                ).then_inc(s["norm2_ready"], 1)

            def norms(group, tmp):
                t0, t1 = EPI[group]
                dve.wait_ge(s["norm2_ready"], group + 1)
                root(number("sd")[:, t0:t1], number("q")[:, t0:t1], tmp).then_inc(s["norm_ready"], 1)

            def time_parts(group, tmp):
                t0, t1 = EPI[group]
                root(number("x0")[:, t0:t1], number("ss")[:, t0:t1], tmp, 1.0 + EPS).then_inc(s["x0_ready"], 1)

            def sinh_factor(group):
                t0, t1 = EPI[group]
                F = {n: number(n)[:, t0:t1] for n in col}
                dve.wait_ge(s["norm_ready"], group + 1)
                L(V.tensor_scalar(F["z"], F["sd"], QKCLIP, None, ALU.min))
                L(V.tensor_tensor(F["m"], F["z"], F["z"], ALU.mult))
                L(V.tensor_scalar(F["a"], F["m"], 1.0 / factorial(2 * K_SINH + 1), None, ALU.mult))
                for k in range(K_SINH - 1, 0, -1):
                    L(V.scalar_tensor_tensor(out=F["a"], in0=F["a"], scalar=1.0 / factorial(2 * k + 1), in1=F["m"],
                                             op0=ALU.add, op1=ALU.mult))
                L(V.scalar_tensor_tensor(out=F["d"], in0=F["a"], scalar=1.0, in1=F["z"], op0=ALU.add, op1=ALU.mult))
                L(V.tensor_scalar(F["dne"], F["z"], EPS, None, ALU.add))
                L(V.reciprocal(F["rec"], F["dne"]))
                L(V.tensor_tensor(F["sc"], F["d"], F["rec"], ALU.mult))

            def scale_clip(t0, t1):
                w = wp[:, t0:t1]
                L(V.tensor_tensor(w, w, number("sc")[:, t0:t1].unsqueeze(2).to_broadcast((P, t1 - t0, D)), ALU.mult))
                L(V.tensor_scalar(w, w, 8.0, -8.0, ALU.min, ALU.max))
                sum_squares(t0, t1)

            def set_time(group):
                t0, t1 = EPI[group]
                dve.wait_ge(s["x0_ready"], group + 1)
                L(V.tensor_copy(wp[:, t0:t1, 0], number("x0")[:, t0:t1]))

            def add_attention(t0, t1):
                L(V.tensor_tensor(xt[:, t0:t1], xt[:, t0:t1], wp[:, t0:t1], ALU.add))

            def add_expert(b, k, half):
                dve.wait_ge(y_back[b], 16 * TOP * JT)
                if k:
                    dve.wait_ge(s["y_added"], 2 * TOP * b + 2)
                y, w = ((y1, "w1"), (y2, "w2"))[k]
                t0 = b * JT + half * HJ
                for t in range(t0, t0 + HJ):
                    ins = V.scalar_tensor_tensor(out=xt[:, t], in0=y[:, t], scalar=number(w)[:, t:t + 1],
                                                 in1=xt[:, t], op0=ALU.mult, op1=ALU.add)
                ins.then_inc(s["y_added"], 1)

            def exp_map_step(st):
                if st in (1, 2, 4, 6):
                    i = (1, 2, 4, 6).index(st)
                    sum_squares(i * HJ, (i + 1) * HJ)
                if st == 6:
                    norm_squares(0)
                if st == 9:
                    sinh_factor(0)
                if st in (10, 12, 14, 17):
                    i = (10, 12, 14, 17).index(st)
                    scale_clip(i * HJ, (i + 1) * HJ)
                if st == 18:
                    dve.sem_inc(s["fss_ready"], 1)
                if st == 20:
                    set_time(0)
                if st in (21, 22):
                    add_attention((st - 21) * JT, (st - 20) * JT)

            def last_iteration_step(st):
                t0, t1 = EPI[1]
                if st in (5, 28):
                    dve.wait_ge(s["lent_read"], lent_base(STAGES[-1], NIT - 1)(
                        sum(len(STAGES[-1].at[i]) for i in range(st))))
                if st == 5:
                    sum_squares(t0, t1)
                    norm_squares(1)
                if st == 6:
                    norms(1, root_tmp)
                if st == 9:
                    sinh_factor(1)
                if st in (10, 11):
                    scale_clip(t0 + (st - 10) * HJ, t0 + (st - 9) * HJ)
                if st == 12:
                    time_parts(1, root_tmp)
                if st == 13:
                    set_time(1)
                    add_attention(t0, t1)
                for b, steps_at in enumerate(ADD_AT):
                    if st in steps_at:
                        i = steps_at.index(st)
                        add_expert(b, i // 2, i % 2)
                    if st == steps_at[-1]:
                        dve.wait_ge(s["y_added"], 2 * TOP * (b + 1))
                        dve.sem_inc(s["out_ready"], 1)
                if st == 28:
                    sum_squares(3 * JT, 3 * JT + HJ)

            def copy_sums(it, n):
                dve.wait_ge(s["pv_done"], affine(it, 4, n + 1))
                V.tensor_copy(osb, bank(O_BANK)).then_inc(s["o_free"], 1)

            def read_sums(it, n):
                o = bank(LENT).rearrange("p (t h r) -> p t h r", t=HJ, h=HG)
                V.reciprocal(orec[:], o[:, :, :, DH]).then_inc(s["o_rec"], 1)
                dve.wait_ge(s["o_rec"], affine(it, 4, n + 1))
                t0 = n % 2 * HJ
                V.tensor_tensor(attn[:, it, n // 2, t0:t0 + HJ, :].rearrange("p t (h c) -> p t h c", h=HG),
                                o[:, :, :, 0:DH], orec[:].unsqueeze(3).to_broadcast((P, HJ, HG, DH)),
                                ALU.mult).then_inc(s["lent_read"], 1)

            def fill_a(hb):
                heads = attn[:].rearrange("p (b a) c (f j) d -> p b a c f j d", a=2, f=2)
                for a in range(2):
                    ins = V.tensor_copy(rows4.rearrange("p j (a c d) -> p a c j d", a=2, c=2)[:, a],
                                        heads[:, hb // 2, a, :, hb % 2])
                ins.then_inc(s["rows_ready"], 1)

            def split_weights(it, n):
                k, (i0, m) = n // 3, IC[n % 3]
                dve.wait_ge(tile_loaded[k % TB], affine(it, 32 * FK // TB, 32 * (k // TB + 1) - FFN0 * 32 * FK // TB))
                w = w_ex[k % TB][:, 0:2 * I].rearrange("p (u i) -> p u i", u=2)[:, :, i0:i0 + m]
                V.tensor_copy(w_hi[:, n % 3, :, 0:m], w).then_inc(s["w_hi_ready"], 1)
                dve.wait_ge(s["w_hi_ready"], affine(it, GU, n + 1 - FFN0 * GU))
                V.tensor_tensor(w_lo[:, n % 3, :, 0:m], w, w_hi[:, n % 3, :, 0:m].bitcast(F32), ALU.subtract
                                ).then_inc(s["w_split"], 1)

            def iteration(sg, it):
                lent = lent_base(sg, it)
                for st in range(STEPS):
                    if st == 0 and sg.carry:
                        copy_sums(it - 1, 3)
                    if st and st % JT == 0:
                        copy_sums(it, st // JT - 1)
                    if st + 1 in sg.gu:
                        split_weights(it, sg.gu[st + 1])
                    for use in sg.at[st]:
                        kind, n = sg.uses[use]
                        dve.wait_ge(s["lent_written"], lent(use + 1))
                        if kind == "x":
                            V.tensor_copy(xs_hi, bank(LENT)[:, 0:ST]).then_inc(s["xs_hi_ready"], 1)
                            dve.wait_ge(s["xs_hi_ready"], affine(it, FK, n + 1 - FFN0 * FK))
                            V.tensor_tensor(xs_lo, bank(LENT)[:, 0:ST], xs_hi.bitcast(F32), ALU.subtract
                                            ).then_inc(s["lent_read"], 1)
                        elif kind == "y":
                            dve.wait_ge(y_stored[n % YB], affine(it, 16 * FK // YB, 16 * (n // YB + 1)
                                                                 - FFN0 * 16 * FK // YB))
                            V.tensor_copy(ys_s[n % YB][:].rearrange("p j d -> p (j d)"), bank(LENT)[:, 0:ST]
                                          ).then_inc(s["lent_read"], 1)
                        elif kind == "o":
                            read_sums(it - 1 if n == 3 else it, n)
                        elif kind in ("vT", "aT"):
                            V.tensor_copy(rT, bank(LENT)).then_inc(s["lent_read"], 1)
                        elif kind == "qkv":
                            if n[1] == 0:
                                dve.wait_ge(s["v_stored"], (it + sg.qkv[n[0]][0]) * 16)
                                dve.wait_ge(s["rest_ready"], it + sg.qkv[n[0]][0])
                            read_qkv(bank(LENT), n[1])
                        elif kind == "part":
                            if n[1] == 0:
                                dve.wait_ge(s["part_stored"], (it + sg.qkv[n[0]][0]) * (32 * NPART))
                            part_copy(bank(LENT, BF16), n[1])
                        elif kind == "logits":
                            keep_logits(n, bank(LENT))
                            dve.wait_ge(s["logits_read"], n + 1)
                            dve.sem_inc(s["lent_read"], 1)
                        else:
                            V.tensor_copy(wproj[:, it + sg.wo[n][0]].rearrange("p j d -> p (j d)"), bank(LENT)
                                          ).then_inc(s["lent_read"], 1)
                    if st in sg.fill:
                        kind, n, offset = sg.fill[st]
                        if kind == "vT":
                            fill_v(it + offset)
                        else:
                            dve.wait_ge(s["lent_read"], lent(sum(len(sg.at[i]) for i in range(st + 1))))
                            fill_a(it + offset)
                    if st - 1 in sg.gu:
                        n = sg.gu[st - 1]
                        m = IC[n % 3][1]
                        gu = bank(GU_BANK + n % 2)
                        dve.wait_ge(s["tanh_done"], affine(it, GU, n + 1 - FFN0 * GU))
                        V.scalar_tensor_tensor(out=ga[0:m, n % 2], in0=th[0:m, n % 2], scalar=1.0, in1=gu[0:m, 0:ST],
                                               op0=ALU.add, op1=ALU.mult).then_inc(s["gate_done"], 1)
                        dve.wait_ge(s["gate_done"], affine(it, GU, n + 1 - FFN0 * GU))
                        V.scalar_tensor_tensor(out=hT[0:m, n // 3 % 2, n % 3], in0=ga[0:m, n % 2], scalar=0.5,
                                               in1=gu[0:m, ST:2 * ST], op0=ALU.mult, op1=ALU.mult
                                               ).then_inc(s["h_ready"], 1)
                    for offset, steps_at, _ in sg.qkv:
                        for part in (SPLIT_DVE if sg.ffn else SPLIT_ALONE).get(st - steps_at[-1], ()):
                            split(part, it + offset)
                    if sg.lo == 0:
                        first_iteration_step(st)
                    if sg.lo == NIT - 2:
                        exp_map_step(st)
                    if sg.last:
                        last_iteration_step(st)

            run(dve, iteration)
            copy_sums(NIT - 1, 3)
            add_expert(B - 1, 0, 0)
            dve.wait_ge(s["lent_written"], LENT_ALL + 1)
            read_sums(NIT - 1, 3)
            dve.wait_ge(s["lent_read"], LENT_ALL + 1)
            fill_a(NHB - 1)
            add_expert(B - 1, 0, 1)
            dve.wait_ge(s["lent_written"], LENT_ALL + 2)
            V.tensor_copy(rT, bank(LENT)).then_inc(s["lent_read"], 1)
            add_expert(B - 1, 1, 0)
            dve.wait_ge(s["lent_written"], LENT_ALL + 3)
            V.tensor_copy(wproj[:, NHB - 1].rearrange("p j d -> p (j d)"), bank(LENT)).then_inc(s["lent_read"], 1)
            dve.wait_ge(s["lent_read"], LENT_ALL + 3)
            sum_squares(3 * JT + HJ, NT)
            norm_squares(2)
            add_expert(B - 1, 1, 1)
            dve.wait_ge(s["y_added"], 2 * TOP * B)
            sinh_factor(2)
            scale_clip(*EPI[2])
            dve.sem_inc(s["fss_ready"], 1)
            set_time(2)
            add_attention(*EPI[2])
            dve.sem_inc(s["out_ready"], 1)

        @block.tensor
        def _(pe):
            M = nc.tensor.matmul

            def transposes(dst, src, n):
                for j in range(n):
                    last = nc.tensor.transpose(dst[:, j * P:(j + 1) * P], src[:, j, :], ident[:])
                return last

            pe.wait_ge(s["consts"], 11)
            pe.wait_ge(s["w_loaded"], 48)

            def turn_xn(b):
                pe.wait_ge(s["xn_ready"], b + 1)
                if b:
                    pe.wait_ge(s["xnT_ready"], 2 * b)
                for half in range(2):
                    transposes(bank(GU_BANK + half), xn_all[:, b, half * HJ:], HJ).then_inc(s["xnT_psum"], 1)

            def logits(b, dst):
                pe.wait_ge(s["xnT_ready"], 2 * b + 2)
                for j in range(JT):
                    last = M(dst[:, j * E:(j + 1) * E], xnT[:, j * P:(j + 1) * P], wr_s[:], start=True, stop=True)
                return last

            turn_xn(0)
            logits(0, bank(0)).then_inc(s["head_logits"], 1)

            def qkv(dst, j):
                return M(dst[:, 0:3 * D], rT[:, j * P:(j + 1) * P], wqkv_s[:], start=True, stop=True)

            def part_transposes(dst, t, hb):
                pe.wait_ge(s[f"p{t}_ready"], hb + 1)
                for w in range(2):
                    for j in range(HJ):
                        last = nc.tensor.transpose(dst[:, (w * HJ + j) * P:(w * HJ + j + 1) * P],
                                                   parts[:, t, j, w * D:(w + 1) * D], identb[:])
                return last

            for u, (kind, hb, n) in enumerate(HEAD_USES):
                free, rows_turned = u - 3, HEAD_USES.index(("vT", hb, 0)) + 1
                need = max(free, rows_turned) if kind == "qkv" else free
                if need > 0:
                    pe.wait_ge(s["lent_read"], need)
                dst = O_BANK + u % 4
                if kind == "vT":
                    pe.wait_ge(s["rows_ready"], hb + 1)
                    last = transposes(bank(dst), rows4, HJ)
                elif kind == "qkv":
                    last = qkv(bank(dst), n)
                else:
                    last = part_transposes(bank(dst, BF16), n, hb)
                last.then_inc(s["lent_written"], 1)

            def rank():
                pe.wait_ge(s["mask_ready"], 1)
                M(bank(GU_BANK)[:, 0:E * NT], ones[:], rt["mask"], start=True, stop=True)
                M(bank(GU_BANK)[:, E * NT:2 * E * NT], tri[:], rt["mask"], start=True, stop=True
                  ).then_inc(s["rank_psum"], 1)

            def weigh(it, st):
                par, kb = st // (2 * JT), st % JT
                if kb == 0:
                    pe.wait_ge(s["o_free"], affine(it, 4, st // JT + 1))
                for h in range(HG):
                    last = M(bank(O_BANK)[32 * h:32 * h + VA, :], vst[par][:, kb, h * VA:(h + 1) * VA],
                             ex[:, st % 2, h, :], start=(kb == 0), stop=(kb == JT - 1))
                if kb == JT - 1:
                    last.then_inc(s["pv_done"], 1)

            def iteration(sg, it):
                lent, rows = lent_base(sg, it), rows_base(sg, it)

                def scores(st):
                    par, qh, kb = st // (2 * JT), st // JT % 2, st % JT
                    if st % (2 * JT) == 0:
                        pe.wait_ge(stack_loaded[par], affine(it, 16 * NSTACK, 16 * NSTACK))
                    for hp in range(2):
                        if st or sg.carry:
                            pe.wait_ge(s["exp_done"], affine(it, 2 * STEPS, 2 * st + hp - 1))
                        for h in (2 * hp, 2 * hp + 1):
                            last = M(ps[:, h, :], kst[par][:, h, kb * P:(kb + 1) * P],
                                     qst[par][:, h, qh * QH:(qh + 1) * QH], start=True, stop=True)
                        last.then_inc(s["scores_ready"], 1)

                def lent_bank(use):
                    kind, n = sg.uses[use]
                    pe.wait_ge(s["lent_read"], lent(use))
                    if kind == "x":
                        pe.wait_ge(tile_loaded[n % TB], affine(it, 32 * FK // TB, 32 * (n // TB + 1)
                                                               - FFN0 * 32 * FK // TB))
                        last = transposes(bank(LENT), xs_s[n % TB], SJ)
                    elif kind == "y":
                        pe.wait_ge(s["h_ready"], affine(it, GU, 3 * n + 3 - FFN0 * GU))
                        for j in range(SJ):
                            for c, (i0, m) in enumerate(IC):
                                last = M(bank(LENT)[:, j * P:(j + 1) * P], hT[0:m, n % 2, c, j * P:(j + 1) * P],
                                         w_ex[n % TB][0:m, 2 * I + c * P:2 * I + (c + 1) * P], start=(c == 0),
                                         stop=(c == 2))
                    elif kind == "o":
                        pe.wait_ge(s["o_free"], affine(it, 4, 1 if n == 3 else n + 2))
                        last = transposes(bank(LENT), osb.rearrange("p (j d) -> p j d", d=P), HJ)
                    elif kind in ("vT", "aT"):
                        pe.wait_ge(s["rows_ready"], rows(sg.filling[kind, n] + 1))
                        last = transposes(bank(LENT), rows4, HJ)
                    elif kind == "qkv":
                        last = qkv(bank(LENT), n[1])
                    elif kind == "part":
                        last = part_transposes(bank(LENT, BF16), n[1], it + sg.qkv[n[0]][0])
                    elif kind == "logits":
                        last = logits(n, bank(LENT))
                    else:
                        last = project()
                    last.then_inc(s["lent_written"], 1)

                def gate_up(n):
                    k, c = n // 3, n % 3
                    m = IC[c][1]
                    if c == 0:
                        pe.wait_ge(s["xs_hi_ready"], affine(it, FK, k + 1 - FFN0 * FK))
                    if n > 1:
                        pe.wait_ge(s["h_ready"], affine(it, GU, n - 1 - FFN0 * GU))
                    pe.wait_ge(s["w_split"], affine(it, GU, n + 1 - FFN0 * GU))
                    for u in range(2):
                        hi, lo = (w[:, n % 3, u, 0:m] for w in (w_hi, w_lo))
                        for i, (w, rows) in enumerate(((hi, xs_hi), (lo, xs_hi), (hi, xs_lo))):
                            if c == 0 and u == 0 and i == 2:
                                pe.wait_ge(s["lent_read"], lent(sg.use("x", k) + 1))
                            last = M(bank(GU_BANK + n % 2)[0:m, u * ST:(u + 1) * ST], w, rows,
                                     start=(i == 0), stop=(i == 2))
                    last.then_inc(s["gu_psum"], 1)

                for st in range(STEPS):
                    scores(st)
                    if st:
                        weigh(it, st - 1)
                    elif sg.carry:
                        weigh(it - 1, STEPS - 1)
                    if st in sg.gu:
                        gate_up(sg.gu[st])
                    for use in sg.at[st]:
                        lent_bank(use)
                    if st in sg.logits:
                        turn_xn(1 + sg.logits.index(st))
                    if sg.lo == 0 and st == RANK_AT:
                        rank()

            def project():
                for j in range(HJ):
                    last = M(bank(LENT)[:, j * P:(j + 1) * P], rT[:, j * P:(j + 1) * P], wo_s[:], start=True, stop=True)
                return last

            run(pe, iteration)
            pe.wait_ge(s["exp_done"], NIT * 2 * STEPS)
            weigh(NIT - 1, STEPS - 1)
            pe.wait_ge(s["lent_read"], LENT_ALL)
            pe.wait_ge(s["o_free"], NIT * 4 + 1)
            transposes(bank(LENT), osb.rearrange("p (j d) -> p j d", d=P), HJ).then_inc(s["lent_written"], 1)
            pe.wait_ge(s["lent_read"], LENT_ALL + 1)
            pe.wait_ge(s["rows_ready"], ROWS_ALL + 1)
            transposes(bank(LENT), rows4, HJ).then_inc(s["lent_written"], 1)
            pe.wait_ge(s["lent_read"], LENT_ALL + 2)
            project().then_inc(s["lent_written"], 1)


def kernel(L0_attn_x, L0_attn_Wq, L0_attn_Wk, L0_attn_Wv, L0_attn_Wo, L0_ffn_w_router, L0_ffn_w_gate, L0_ffn_w_up,
           L0_ffn_w_down):
    import concourse.bacc as bacc
    from concourse.bass_utils import run_bass_kernel_spmd

    a = [np.asarray(v) for v in (L0_attn_x, L0_attn_Wq, L0_attn_Wk, L0_attn_Wv, L0_attn_Wo, L0_ffn_w_router,
                                 L0_ffn_w_gate, L0_ffn_w_up, L0_ffn_w_down)]
    x, wq, wk, wv, wo, wr, wg, wu, wd = a
    gch = lambda w: w.reshape(GB, HG, DH, D).transpose(0, 2, 1, 3).reshape(D, D).T
    wqkv = np.concatenate([gch(wq), gch(wk), wv.T], axis=1)
    down = np.zeros((E, 3 * P, D), wd.dtype)
    down[:, :I] = wd.transpose(0, 2, 1)
    down = down.reshape(E, 3, P, D).transpose(0, 2, 1, 3).reshape(E, P, 3 * D)
    wpack = np.concatenate([wg.transpose(0, 2, 1), wu.transpose(0, 2, 1), down], axis=2)
    arrays = {"x": x, "wqkv": wqkv, "wo": wo.T, "wr": wr.T, "wpack": wpack}
    arrays = {k: np.ascontiguousarray(v) for k, v in arrays.items()}

    nc = bacc.Bacc("TRN2", target_bir_lowering=False, num_devices=1)
    aps = [nc.dram_tensor(k, v.shape, mybir.dt.from_np(v.dtype), kind="ExternalInput").ap() for k, v in arrays.items()]
    out = nc.dram_tensor("out", (B, S, D), F32, kind="ExternalOutput").ap()
    block_program(nc, *aps, out)
    r = run_bass_kernel_spmd(nc, [arrays], core_ids=[0])
    return r.results[0]["out"]
```
